# Optimizing a Trainium2 kernel written in Bass

```python
import numpy as np
import jax
import jax.numpy as jnp

def _softmax(x, axis=-1):
    return jax.nn.softmax(x, axis=axis)
def _gelu(x):
    return jax.nn.gelu(x, approximate=True)
def _silu(x):
    return jax.nn.silu(x)
def _sigmoid(x):
    return jax.nn.sigmoid(x)
def _layernorm(x, axis=-1, eps=1e-5):
    m = jnp.mean(x, axis=axis, keepdims=True)
    v = jnp.var(x, axis=axis, keepdims=True)
    return (x - m) / jnp.sqrt(v + eps)
def _scatter_add(tgt, idx, src, axis=0):
    return tgt.at[idx].add(src)
def _segment_sum(src, seg, n):
    return jax.ops.segment_sum(src, seg, n)

kernel_name = 'mk_adj_seq_d1_adj_512_18ca49'

def setup_inputs(seed: int = 0):
    np.random.seed(seed)
    _w = jnp.asarray
    def _rec_inputs():
        import jax
        import jax.numpy as jnp
        _gk = jax.random.key(seed)
        x = -0.0005207 + 1.001 * jax.random.normal(jax.random.fold_in(_gk, 1), (8192, 512), jnp.float32)
        _a = jax.random.bernoulli(jax.random.fold_in(_gk, 2), 0.00195312, (8192, 8192))
        adj = _a.astype(jnp.int32)
        return x, adj
    x, adj = _rec_inputs()
    def _L0_gnn_setup():
        import jax, jax.numpy as jnp
        import numpy as np
        N, DIM = (4096, 512)
        F_OUT = DIM // 8
        HID = int(DIM * 2.0)
        ALPHA = 0.2
        MASK_VAL = -9000000000000000.0

        def _layernorm(x, g, b, eps=1e-05):
            mu = x.mean(-1, keepdims=True)
            var = ((x - mu) ** 2).mean(-1, keepdims=True)
            return (x - mu) * jax.lax.rsqrt(var + eps) * g + b
        key = jax.random.key(seed)
        ks = jax.random.split(key, 8)
        x = jax.random.normal(ks[0], (N, DIM), jnp.float32)
        adj = jax.random.randint(ks[1], (N, N), 0, 2, jnp.int32)
        W = jax.random.normal(ks[2], (DIM, F_OUT), jnp.float32) * 0.1
        a = jax.random.normal(ks[3], (2 * F_OUT, 1), jnp.float32) * 0.1
        fc_w = jax.random.normal(ks[4], (DIM, F_OUT), jnp.float32) * 0.1
        fc_b = jnp.zeros((DIM,), jnp.float32)
        ln1_g = jnp.ones((DIM,), jnp.float32)
        ln1_b = jnp.zeros((DIM,), jnp.float32)
        ln2_g = jnp.ones((DIM,), jnp.float32)
        ln2_b = jnp.zeros((DIM,), jnp.float32)
        fc1_w = jax.random.normal(ks[5], (HID, DIM), jnp.float32) * 0.05
        fc1_b = jnp.zeros((HID,), jnp.float32)
        fc2_w = jax.random.normal(ks[6], (DIM, HID), jnp.float32) * 0.05
        fc2_b = jnp.zeros((DIM,), jnp.float32)
        return dict(x=x, adj=adj, W=W, a=a, fc_w=fc_w, fc_b=fc_b, ln1_g=ln1_g, ln1_b=ln1_b, ln2_g=ln2_g, ln2_b=ln2_b, fc1_w=fc1_w, fc1_b=fc1_b, fc2_w=fc2_w, fc2_b=fc2_b)
    _L0_gnn_all = _L0_gnn_setup()
    _L0_gnn_in = {k: v for k, v in _L0_gnn_all.items() if k in ('W', 'a', 'fc_w', 'fc_b', 'ln1_g', 'ln1_b', 'ln2_g', 'ln2_b', 'fc1_w', 'fc1_b', 'fc2_w', 'fc2_b', )}
    del _L0_gnn_all

    return {
        "x": x,
        "adj": adj,
        "L0_gnn_W": _L0_gnn_in["W"],
        "L0_gnn_a": _L0_gnn_in["a"],
        "L0_gnn_fc_w": _L0_gnn_in["fc_w"],
        "L0_gnn_fc_b": _L0_gnn_in["fc_b"],
        "L0_gnn_ln1_g": _L0_gnn_in["ln1_g"],
        "L0_gnn_ln1_b": _L0_gnn_in["ln1_b"],
        "L0_gnn_ln2_g": _L0_gnn_in["ln2_g"],
        "L0_gnn_ln2_b": _L0_gnn_in["ln2_b"],
        "L0_gnn_fc1_w": _L0_gnn_in["fc1_w"],
        "L0_gnn_fc1_b": _L0_gnn_in["fc1_b"],
        "L0_gnn_fc2_w": _L0_gnn_in["fc2_w"],
        "L0_gnn_fc2_b": _L0_gnn_in["fc2_b"],
    }

def reference(x, adj, L0_gnn_W, L0_gnn_a, L0_gnn_fc_w, L0_gnn_fc_b, L0_gnn_ln1_g, L0_gnn_ln1_b, L0_gnn_ln2_g, L0_gnn_ln2_b, L0_gnn_fc1_w, L0_gnn_fc1_b, L0_gnn_fc2_w, L0_gnn_fc2_b):
    import jax
    import jax.numpy as jnp
    def _L0_gnn_ref(x, adj, W, a, fc_w, fc_b, ln1_g, ln1_b, ln2_g, ln2_b, fc1_w, fc1_b, fc2_w, fc2_b):
        import jax, jax.numpy as jnp
        import numpy as np
        N, DIM = (4096, 512)
        F_OUT = DIM // 8
        HID = int(DIM * 2.0)
        ALPHA = 0.2
        MASK_VAL = -9000000000000000.0

        def _layernorm(x, g, b, eps=1e-05):
            mu = x.mean(-1, keepdims=True)
            var = ((x - mu) ** 2).mean(-1, keepdims=True)
            return (x - mu) * jax.lax.rsqrt(var + eps) * g + b
        h = _layernorm(x, ln1_g, ln1_b)
        Wh = h @ W
        f_src = Wh @ a[:F_OUT, 0]
        f_dst = Wh @ a[F_OUT:, 0]
        e = f_src[:, None] + f_dst[None, :]
        e = jnp.where(e >= 0, e, ALPHA * e)
        att = jax.nn.softmax(jnp.where(adj > 0, e, MASK_VAL), axis=1)
        h_prime = att @ Wh
        attn_out = h_prime @ fc_w.T + fc_b
        x = x + attn_out
        h2 = _layernorm(x, ln2_g, ln2_b)
        m = jax.nn.gelu(h2 @ fc1_w.T + fc1_b, approximate=False)
        m = m @ fc2_w.T + fc2_b
        return x + m

    x = _L0_gnn_ref(x, adj, L0_gnn_W, L0_gnn_a, L0_gnn_fc_w, L0_gnn_fc_b, L0_gnn_ln1_g, L0_gnn_ln1_b, L0_gnn_ln2_g, L0_gnn_ln2_b, L0_gnn_fc1_w, L0_gnn_fc1_b, L0_gnn_fc2_w, L0_gnn_fc2_b)
    return x


_drawn_inputs = setup_inputs


def setup_inputs(seed=0):
    import zlib

    import numpy as np

    out = dict(_drawn_inputs(seed))
    spreads = {'L0_gnn_fc_b': (0.0, 0.1),
     'L0_gnn_ln1_g': (1.0, 0.2),
     'L0_gnn_ln1_b': (0.0, 0.1),
     'L0_gnn_ln2_g': (1.0, 0.2),
     'L0_gnn_ln2_b': (0.0, 0.1),
     'L0_gnn_fc1_b': (0.0, 0.1),
     'L0_gnn_fc2_b': (0.0, 0.1)}
    factors = {}
    for name, (base, spread) in spreads.items():
        noise = np.random.default_rng([zlib.crc32(name.encode()), seed]).standard_normal(out[name].shape)
        drawn = base * np.exp(spread * noise) if base else spread * noise
        out[name] = jnp.asarray(drawn.astype(out[name].dtype))
    for name, factor in factors.items():
        out[name] = (out[name] * factor).astype(out[name].dtype)
    return out
```

```python
from contextlib import ExitStack

import concourse.bass as bass
from concourse import mybir

F32 = mybir.dt.float32
F32R = mybir.dt.float32r
BF16 = mybir.dt.bfloat16
I32 = mybir.dt.int32
I8 = mybir.dt.int8
U8 = mybir.dt.uint8
U32 = mybir.dt.uint32
FP8 = mybir.dt.float8e4
ALU = mybir.AluOpType
ACT = mybir.ActivationFunctionType
AX_X = mybir.AxisListType.X
RMAX = bass.bass_isa.ReduceOp.max

P = 128
Q = 32
SLOPE = 0.2
EPS = 1e-5
HEADROOM = 48.0
EDGE_BYTE = 0x40
EDGE_WORD = 0x40404040


class Steps:

    def __init__(self, eng, sem, before):
        self.eng, self.sem, self.n = eng, sem, before

    def did(self, ins):
        ins.then_inc(self.sem, 1)
        self.n = self.n + 1

    def wait(self):
        self.eng.wait_ge(self.sem, self.n)


def in_register(eng, value):
    return value if isinstance(value, int) else eng.snap(value)


def gat_layer(nc, x, adj, W, a, fc_wT, fc_b, ln1_g, ln1_b, ln2_g, ln2_b, fc1_wT, fc1_b, fc2_wT, fc2_b, out):
    N, D = x.shape
    F = W.shape[1]
    HID = fc1_wT.shape[1]
    KC = D // P
    HC = HID // P
    C1 = F + 1
    PART = 3 * C1
    NB = N // 512
    SUB = 4
    NBL = 16
    STG = 4
    QC = N // 4
    NT = N // P
    RING = 2
    BYTES = 2
    CR = 4
    EV = 14
    LN = 7
    assert D == 512 and F == 64 and HID == 1024 and N == 8192

    s_dram = nc.dram_tensor("f_src_rows", [1, N], F32).ap()

    with ExitStack() as ctx:
        def sb(name, shape, dt):
            return ctx.enter_context(nc.sbuf_tensor(name, shape, dt))

        def sem(name):
            return ctx.enter_context(nc.semaphore(name))

        uv = sb("uv", [P, NT, 2 * PART], BF16)
        w1h = sb("w1h", [P, KC, HID], F32R)
        w1l = sb("w1l", [P, KC, HID], F32R)
        w2h = sb("w2h", [P, HC, D], F32R)
        w2l = sb("w2l", [P, HC, D], F32R)
        fch = sb("fch", [P, D], F32R)
        fcl = sb("fcl", [P, D], F32R)
        adj_ring = sb("adj_ring", [P, RING, 2048], I32)
        byte_ring = sb("byte_ring", [P, BYTES, 2048], U8)
        edges = sb("edges", [P, 2, 2048], U32)
        signs = sb("signs", [P, CR, 512], U32)
        xrows = sb("xrows", [P, SUB, D], F32)
        work = sb("work", [P, 2080], F32)
        h2h = sb("h2h", [P, KC, 256], F32R)
        h2l = sb("h2l", [P, KC, 256], F32R)
        m_f = sb("m_f", [P, 2, 256], F32)
        m_h = sb("m_h", [P, 2, 256], F32R)
        m_l = sb("m_l", [P, 2, 256], F32R)
        srows = sb("srows", [P, 2, 512], F32)
        hcat = sb("hcat", [P, SUB, P], F32R)
        hT = sb("hT", [P, SUB * P], F32R)
        biases = sb("biases", [3, 2, D], BF16)
        ones3 = sb("ones3", [3, P], BF16)
        ident = sb("ident", [P, P], F32)
        ones = sb("ones", [P, P], F32)
        wsum = sb("wsum", [P, F], F32)
        s_tab = sb("s_tab", [P, NT], F32)
        nd_tab = sb("nd_tab", [P, NT], F32)
        u_tab = sb("u_tab", [P, NT, 2], F32)
        ab_tab = sb("ab_tab", [P, NT, 2], F32)
        c1 = sb("c1", [P, HC], F32)
        b1c = sb("b1c", [P, HC], F32)
        lnc = sb("lnc", [P, 4, KC], F32)
        stat = sb("stat", [P, 4, 6], F32)
        mv = sb("mv", [P, 2, 4, 2], F32)
        rstd = sb("rstd", [P, 2, 4], F32)
        mv2 = sb("mv2", [P, 2, 2], F32)
        rstd2 = sb("rstd2", [P, 2], F32)
        mhalf = sb("mhalf", [P, 4], F32)
        eps = sb("eps", [P, 4], F32)
        dmax = sb("dmax", [P, 4], F32)
        den = sb("den", [P, 3, SUB], F32)

        acc = ctx.enter_context(nc.psum_tensor("acc", [P, SUB, 512], F32))
        rowp = ctx.enter_context(nc.psum_tensor("rowp", [P, 2, 512], F32))
        turn = ctx.enter_context(nc.psum_tensor("turn", [P, 2, 512], F32))

        whs = edges[:, :, :].bitcast(F32).rearrange("p a b -> p (a b)").rearrange("p (t f) -> p t f", f=F)
        xin = [
            adj_ring[:, 0, :].bitcast(F32), adj_ring[:, 1, :].bitcast(F32),
            xrows[:, :, :].rearrange("p a b -> p (a b)"), work[:, 0:2048],
        ]
        xT = signs[:, :, :].bitcast(F32)
        wx = m_f[:, :, :].rearrange("p a b -> p (a b)")[:, 0:KC * 66].rearrange("p (c f) -> p c f", c=KC)
        wraw = srows[:, 0, 0:KC * F].rearrange("p (c f) -> p c f", c=KC)
        wprod = srows[:, 0, 256:512].rearrange("p (c f) -> p c f", c=KC)
        a_bc = srows[:, 1, 0:2 * F]
        crow = srows[:, 1, 128:194]
        b1rep = xT[:, 3, :].rearrange("p (c m) -> p c m", c=KC)
        snat = m_f[0:NT, 0, 0:P]
        t_tab, lt_tab = m_f[:, 1, 128:128 + NT], m_f[:, 1, 192:192 + NT]
        ef = edges[:, :, :].bitcast(F32)
        brow = ef[0:1, 0, 0:2 * D]
        bparts = edges[:, :, :].bitcast(BF16)[0:1, 1, 0:6 * D].rearrange("a (t v d) -> a t v d", t=3, v=2)
        fcs = ef[:, 1, 1536:2048]

        xhat = work[:, 0:1024].rearrange("p (t d) -> p t d", t=2)
        red = work[:, 1024:1544].rearrange("p (s v c) -> p s v c", s=SUB, v=2)
        num = work[:, 1544:1804].rearrange("p (s c) -> p s c", s=SUB)
        hp = work[:, 1804:2060].rearrange("p (s c) -> p s c", s=SUB)
        uf = [work[:, v * 1040:(v + 1) * 1040].rearrange("p (t c) -> p t c", t=16) for v in range(2)]
        eb = edges[:, :, :].bitcast(FP8).rearrange("p g (b i k) -> p g b i k", b=4, k=4)
        sbm = signs[:, :, :].bitcast(FP8).rearrange("p c (i k) -> p c i k", k=4)
        sbu = signs[:, :, :].bitcast(U8).rearrange("p c (i k) -> p c i k", k=4)
        accp = acc[:, :, 0:2 * PART].rearrange("p s (v t c) -> p s v c t", v=2, t=3)

        const_landed = sem("const_landed")
        const_made = sem("const_made")
        prep_step = sem("prep_step")
        prep_sums = sem("prep_sums")
        xin_landed = [sem(f"xin_landed{i}") for i in range(4)]
        stats_step = sem("stats_step")
        aggr_begun = sem("aggr_begun")
        stats_done = sem("stats_done")
        var_step = sem("var_step")
        rstd_ready = sem("rstd_ready")
        xhat_done = sem("xhat_done")
        x_turned = sem("x_turned")
        xT_ready = sem("xT_ready")
        wh_done = sem("wh_done")
        wh_ready = sem("wh_ready")
        table_step = sem("table_step")
        s_stored = sem("s_stored")
        s_landed = sem("s_landed")
        dmax_ready = sem("dmax_ready")
        s_turned = sem("s_turned")
        wsum_done = sem("wsum_done")
        exps_done = sem("exps_done")
        uv_rest = sem("uv_rest")
        uv_part = sem("uv_part")
        srow_landed = sem("srow_landed")
        bias_step = sem("bias_step")
        bias_landed = sem("bias_landed")
        piece_landed = [sem(f"piece_landed{i}") for i in range(RING)]
        bytes_ready = sem("bytes_ready")
        turned = sem("turned")
        mask_step = sem("mask_step")
        masks_taken = sem("masks_taken")
        masks_used = sem("masks_used")
        evac_step = sem("evac_step")
        h_turned = sem("h_turned")
        hT_ready = sem("hT_ready")
        fc_done = sem("fc_done")
        ln_step = sem("ln_step")
        var2_step = sem("var2_step")
        rstd2_ready = sem("rstd2_ready")
        h2_turned = sem("h2_turned")
        h2h_ready = sem("h2h_ready")
        h2l_ready = sem("h2l_ready")
        fc1_done = sem("fc1_done")
        gelu_done = sem("gelu_done")
        m_ready = sem("m_ready")
        fc2_done = sem("fc2_done")
        out_added = sem("out_added")
        stored = [sem(f"stored{i}") for i in range(2)]
        x_landed = [sem(f"x_landed{i}") for i in range(2)]
        w_landed = [sem(f"w_landed{i}") for i in range(4)]
        w_split = sem("w_split")
        c1_done = sem("c1_done")
        c1_ready = sem("c1_ready")

        CONSTS = 16 * 11
        block = ctx.enter_context(nc.Block())

        @block.sync
        def _(sp):
            sp.dma_start(wraw, W.rearrange("(c p) f -> p c f", p=P)).then_inc(const_landed, 16)
            sp.dma_start(a_bc, a.to_broadcast([P, 2 * F])).then_inc(const_landed, 16)
            for i, v in enumerate((ln1_g, ln1_b, ln2_g, ln2_b)):
                sp.dma_start(lnc[:, i, :], v).then_inc(const_landed, 16)
            sp.dma_start(b1c[:], fc1_b).then_inc(const_landed, 16)

            def load_xin(b, u):
                for q in range(4):
                    sp.dma_start(xin[u][Q * q:Q * q + Q, :],
                                 x[bass.ds(QC * q + P * b, P), :].rearrange("(p k) d -> p (k d)", k=4))\
                      .then_inc(xin_landed[u], 16)

            for u in range(4):
                load_xin(u, u)
            sp.dma_start(brow[:, 0:D], fc_b).then_inc(const_landed, 16)
            sp.dma_start(brow[:, D:2 * D], fc2_b).then_inc(const_landed, 16)
            for h in range(2):
                sp.dma_start(fcs[F * h:F * h + F, :], fc_wT).then_inc(const_landed, 16)
            sp.wait_ge(bias_step, 5)
            for t in range(3):
                sp.dma_start(biases[t:t + 1, :, :], bparts[:, t, :, :]).then_inc(bias_landed, 16)

            with sp.Fori(1, 4) as i:
                for u in range(4):
                    used = in_register(sp, 16 * i + (4 * u - 12))
                    sp.wait_ge(x_turned, used)
                    load_xin(4 * i + u, u)

            sp.wait_ge(wh_ready, NBL)
            for q in range(4):
                sp.dma_start(s_dram[0:1, QC * q:QC * q + QC].rearrange("a (b p k) -> (a p) b k", p=Q, k=4),
                             s_tab[Q * q:Q * q + Q, :].rearrange("p (b k) -> p b k", k=4)).then_inc(s_stored, 16)
            sp.wait_ge(s_stored, 64)
            sp.dma_start(snat, s_dram.rearrange("a (t p) -> (a t) p", p=P)).then_inc(s_landed, 16)

            def load_srows(n):
                sp.dma_start(srows[:, n % 2, :], s_dram[0:1, bass.ds(n * 512, 512)].to_broadcast([P, 512]))\
                  .then_inc(srow_landed, 16)

            load_srows(0)

            def load_piece(n, i):
                for q in range(4):
                    col = QC * q + 512 * (i // SUB)
                    sp.dma_start(adj_ring[Q * q:Q * q + Q, i % RING, :].rearrange("r (g c) -> r g c", g=4),
                                 adj[bass.ds(n * 512 + (i % SUB) * P, P), col:col + 512]
                                 .rearrange("(g r) c -> r g c", r=Q)).then_inc(piece_landed[i % RING], 16)

            for i in range(8):
                if i >= RING:
                    sp.wait_ge(bytes_ready, i - RING + 1)
                load_piece(0, i)

            def load_w(j):
                src = fc1_wT[P * (j // 2):P * (j // 2) + P, 512 * (j % 2):512 * (j % 2) + 512] if j < 8 \
                    else fc2_wT[P * (j - 8):P * (j - 8) + P, :]
                sp.dma_start(xrows[:, j % 4, :], src).then_inc(w_landed[j % 4], 16)

            def load_x(m, p):
                sp.dma_start(xrows[:, 2 * p:2 * p + 2, :],
                             x[bass.ds(m * 512 + p * 256, 256), :].rearrange("(t p) d -> p t d", p=P))\
                  .then_inc(x_landed[p], 16)

            def store(m, p):
                sp.dma_start(out[bass.ds(m * 512 + p * 256, 256), :].rearrange("(t p) d -> p t d", p=P),
                             xrows[:, 2 * p:2 * p + 2, :]).then_inc(stored[p], 16)

            def ahead(n, j, last=False):
                if not (last and j >= 8):
                    due = in_register(sp, 16 * n + (j + 9 - RING))
                    sp.wait_ge(bytes_ready, due)
                    load_piece(n + (j + 8) // 16, (j + 8) % 16)
                if j == 4 and not last:
                    made = in_register(sp, 48 * n + 3)
                    sp.wait_ge(mask_step, made)
                    load_srows(n + 1)

            for j in range(16):
                ahead(0, j)
                if j == 0:
                    sp.wait_ge(x_turned, NT)
                if j >= 4:
                    sp.wait_ge(w_split, 2 * (j - 4) + 2)
                if 4 <= j < 12:
                    sp.wait_ge(c1_done, j - 3)
                load_w(j)
            sp.wait_ge(w_split, 2 * 16)
            load_x(0, 0)
            load_x(0, 1)

            def iteration(n, first=False, last=False):
                m = n - 1
                for j in range(16):
                    ahead(n, j, last)
                    if j == 1 and not first:
                        due = in_register(sp, 2 * n - 2)
                        sp.wait_ge(out_added, due)
                        store(n - 2, 1)
                    if j == 4 and not first:
                        due = in_register(sp, 16 * n - 16)
                        sp.wait_ge(stored[1], due)
                        load_x(n - 1, 1)
                    if j == 9:
                        due = in_register(sp, 2 * n - 1)
                        sp.wait_ge(out_added, due)
                        store(n - 1, 0)
                    if j == 12:
                        due = in_register(sp, 16 * n)
                        sp.wait_ge(stored[0], due)
                        load_x(n, 0)

            iteration(1, first=True)
            with sp.Fori(2, NB - 1) as n:
                iteration(n)
            iteration(NB - 1, last=True)
            sp.wait_ge(out_added, 2 * NB - 2)
            store(NB - 2, 1)
            sp.wait_ge(stored[1], 16 * (NB - 1))
            load_x(NB - 1, 1)
            sp.wait_ge(out_added, 2 * NB - 1)
            store(NB - 1, 0)
            sp.wait_ge(out_added, 2 * NB)
            store(NB - 1, 1)
            for p in range(2):
                sp.wait_ge(stored[p], 16 * NB)

        @block.gpsimd
        def _(pool):
            pool.memset(mhalf[:], -0.5)
            pool.memset(eps[:], EPS)
            pool.memset(ones[:], 1.0).then_inc(const_made, 1)
            pool.wait_ge(const_made, 1)
            pool.affine_select(out=ident[:], in_=ones[:], compare_op=ALU.is_equal, fill=0.0, base=0,
                               pattern=[[-1, P]], channel_multiplier=1).then_inc(const_made, 1)

            def rstd_of(b, s):
                pool.wait_ge(stats_done, b + 1)
                pool.tensor_tensor(rstd[:, s, :], mv[:, s, :, 1], eps[:], ALU.add).then_inc(var_step, 1)
                pool.wait_ge(var_step, b + 1)
                pool.tensor_tensor(rstd[:, s, :], rstd[:, s, :], mhalf[:], ALU.pow).then_inc(rstd_ready, 1)

            with pool.Fori(0, NBL // 2) as i:
                for s in range(2):
                    rstd_of(2 * i + s, s)

            pool.wait_ge(table_step, 2)
            pool.partition_all_reduce(dmax[:, 1:2], dmax[:, 0:1], P, RMAX).then_inc(dmax_ready, 1)

            with pool.Fori(0, 2 * NB) as g:
                pool.wait_ge(ln_step, LN * g + 5)
                pool.tensor_tensor(rstd2[:], mv2[:, :, 1], eps[:, 0:2], ALU.add).then_inc(var2_step, 1)
                pool.wait_ge(var2_step, g + 1)
                pool.tensor_tensor(rstd2[:], rstd2[:], mhalf[:, 0:2], ALU.pow).then_inc(rstd2_ready, 1)

        @block.scalar
        def _(act):
            act.wait_ge(prep_sums, 1)

            def move_xT(b, k):
                act.wait_ge(x_turned, 4 * b + (k + 1))
                act.activation(xT[:, k, :], turn[:, k % 2, :], ACT.Copy).then_inc(xT_ready, 1)

            with act.Fori(0, NBL) as b:
                for k in range(4):
                    move_xT(b, k)

            act.wait_ge(table_step, 4)
            act.activation(u_tab[:, :, 0], nd_tab[:], ACT.Exp, scale=-1.0, bias=dmax[:, 2:3])
            act.activation(u_tab[:, :, 1], nd_tab[:], ACT.Exp, scale=-SLOPE, bias=dmax[:, 3:4]).then_inc(exps_done, 1)
            act.wait_ge(table_step, 8)
            act.activation(ab_tab[:], ab_tab[:], ACT.Exp).then_inc(exps_done, 1)

            for st in range(STG):
                for t in range(3):
                    for v in range(2):
                        act.wait_ge(uv_rest, 6 * st + 2 * t + v + 1)
                        c = PART * v + C1 * t
                        act.activation(uv[:, 16 * st:16 * st + 16, c:c + C1], uf[v], ACT.Copy).then_inc(uv_part, 1)
            act.activation(rstd[:, 0, :], mhalf[:], ACT.Gelu)

            def to_bytes(n, i):
                due = n * 16 + (i + 1)
                slot, at = i % RING, i % BYTES
                act.wait_ge(piece_landed[slot], 64 * (8 * n + (i // RING + 1)))
                if not (isinstance(n, int) and n * 16 + i < BYTES):
                    act.wait_ge(turned, 16 * n + (i + 1 - BYTES))
                act.activation(byte_ring[:, at, :].bitcast(I8), adj_ring[:, slot, :], ACT.Sign, scale=-1.0, bias=0.5)\
                   .then_inc(bytes_ready, 1)

            for i in range(6):
                to_bytes(0, i)

            def ahead(n, j, last=False):
                if not (last and j >= 10):
                    to_bytes(n + (j + 6) // 16, (j + 6) % 16)

            def move_hT(m):
                act.wait_ge(h_turned, m + 1)
                act.activation(hT[:], turn[:, 0, :], ACT.Copy).then_inc(hT_ready, 1)

            def move_h2(m, p):
                for c in range(2):
                    act.wait_ge(h2_turned, 4 * m + (2 * p + c + 1))
                    act.activation(h2h[:, 2 * c:2 * c + 2, :].rearrange("p c i -> p (c i)"), turn[:, c, :], ACT.Copy)\
                       .then_inc(h2h_ready, 1)

            def gelu(m, p, h):
                act.wait_ge(fc1_done, 16 * m + (8 * p + h + 1))
                act.activation(m_f[:, h % 2, :], turn[:, h % 2, 0:256], ACT.Gelu, bias=c1[:, h:h + 1])
                act.activation(m_h[:, h % 2, :], turn[:, h % 2, 0:256], ACT.Gelu, bias=c1[:, h:h + 1])\
                   .then_inc(gelu_done, 1)

            def rows(m, j):
                p, l = j // 8, j % 8
                if j == 0:
                    move_hT(m)
                if l == 3:
                    move_h2(m, p)
                if l >= 4:
                    gelu(m, p, 2 * l - 8)
                    gelu(m, p, 2 * l - 7)

            for j in range(16):
                ahead(0, j)
            act.wait_ge(c1_ready, 1)
            with act.Fori(1, NB - 1) as n:
                for j in range(16):
                    ahead(n, j)
                    rows(n - 1, j)
            for j in range(16):
                ahead(NB - 1, j, last=True)
                rows(NB - 2, j)
            for j in range(16):
                rows(NB - 1, j)

        @block.tensor
        def _(pe):
            pe.wait_ge(prep_step, 6)
            for c in range(KC):
                mm = pe.matmul(rowp[:, 0, 0:66], b1rep[:, c, :], wx[:, c, :], start=(c == 0), stop=(c == KC - 1))
            mm.then_inc(prep_sums, 1)
            pe.wait_ge(prep_step, 11)
            pe.wait_ge(const_made, 2)

            def project_x(b, u, k):
                pe.wait_ge(xT_ready, 4 * b + (k + 1))
                for c in range(KC):
                    mm = pe.matmul(rowp[:, u % 2, 66 * k:66 * k + 66], xT[:, k, P * c:P * c + P], wx[:, c, :],
                                   start=(k == 0 and c == 0), stop=(c == KC - 1), skip_group_check=True)
                if k == 3:
                    mm.then_inc(wh_done, 1)

            def piece(b, u, before):
                for k in range(4):
                    pe.wait_ge(xhat_done, 4 * b + (k + 1))
                    for c in range(KC):
                        at = 512 * k + P * c
                        mm = pe.transpose(turn[:, k % 2, P * c:P * c + P], xin[u][:, at:at + P], ident[:])
                    mm.then_inc(x_turned, 1)
                    if k:
                        project_x(b, u, k - 1)
                    elif before:
                        project_x(b - 1, u - 1, 3)
                if before:
                    pe.wait_ge(wh_ready, b)

            piece(0, 0, False)
            for u in range(1, 4):
                piece(u, u, True)
            with pe.Fori(1, 4) as i:
                for u in range(4):
                    piece(4 * i + u, u, True)
            project_x(NBL - 1, 3, 3)

            pe.wait_ge(s_landed, 16)
            pe.transpose(acc[:, 0, 0:NT], snat, ident[0:NT, 0:NT]).then_inc(s_turned, 1)
            pe.wait_ge(wh_ready, NBL)
            for g in range(8):
                mm = pe.matmul(acc[:, 1, :], ones[:], whs[:, 8 * g:8 * g + 8, :].rearrange("p t f -> p (t f)"),
                               start=(g == 0), stop=(g == 7))
            mm.then_inc(wsum_done, 1)
            pe.wait_ge(table_step, 9)

            def attend(n, b):
                if b == 0 and not (isinstance(n, int) and n == 0):
                    pe.wait_ge(evac_step, EV * n + (4 - EV))
                pe.wait_ge(mask_step, 48 * n + (3 * b + 3))
                pe.sem_inc(masks_taken, 1)
                if isinstance(n, int) and n == 0:
                    pe.wait_ge(uv_part, 6 * (b // 4) + 6)
                for s in range(SUB):
                    for k in range(4):
                        c = 4 * b + k
                        pe.matmul(acc[:, s, 0:PART], eb[:, (b // 4) % 2, b % 4, P * s:P * s + P, k], uv[:, c, 0:PART],
                                  start=(c == 0), stop=(c == NT - 1), skip_group_check=True)
                        mm = pe.matmul(acc[:, s, PART:2 * PART], sbm[:, b % CR, P * s:P * s + P, k],
                                       uv[:, c, PART:2 * PART], start=False, stop=(c == NT - 1), skip_group_check=True)
                mm.then_inc(masks_used, 1)

            def turn_h(m):
                pe.wait_ge(evac_step, EV * m + EV)
                for s in range(SUB):
                    mm = pe.transpose(turn[:, 0, P * s:P * s + P], hcat[:, s, :].bitcast(F32), ident[:])
                mm.then_inc(h_turned, 1)

            def fc(m, p):
                pe.wait_ge(hT_ready, m + 1)
                if not (isinstance(m, int) and m == 0 and p == 0):
                    pe.wait_ge(out_added, 2 * m + p)
                for t in range(2):
                    rows = hT[:, P * (2 * p + t):P * (2 * p + t) + P]
                    pe.matmul(rowp[:, t, :], rows, fch[:], start=True, stop=False)
                    pe.matmul(rowp[:, t, :], rows, fcl[:], start=False, stop=False)
                    mm = pe.matmul(rowp[:, t, :], ones3[:], biases[:, 0, :], start=False, stop=True)
                mm.then_inc(fc_done, 1)

            def turn_h2(m, p):
                pe.wait_ge(ln_step, 2 * LN * m + (LN * p + LN))
                for c in range(KC):
                    for t in range(2):
                        at = 256 * (c % 2) + P * t
                        mm = pe.transpose(turn[:, c // 2, at:at + P], xhat[:, t, P * c:P * c + P], ident[:])
                    if c % 2:
                        mm.then_inc(h2_turned, 1)

            def fc1(m, p, h):
                pe.wait_ge(h2l_ready, 4 * m + (2 * p + 2))
                for c in range(KC):
                    w, wl = w1h[:, c, P * h:P * h + P], w1l[:, c, P * h:P * h + P]
                    pe.matmul(turn[:, h % 2, 0:256], w, h2h[:, c, :], start=(c == 0), stop=False)
                    pe.matmul(turn[:, h % 2, 0:256], w, h2l[:, c, :], start=False, stop=False)
                    mm = pe.matmul(turn[:, h % 2, 0:256], wl, h2h[:, c, :], start=False, stop=(c == KC - 1))
                mm.then_inc(fc1_done, 1)

            def fc2(m, p, h):
                pe.wait_ge(m_ready, 16 * m + (8 * p + h + 1))
                for t in range(2):
                    hi, lo = m_h[:, h % 2, P * t:P * t + P], m_l[:, h % 2, P * t:P * t + P]
                    pe.matmul(rowp[:, t, :], hi, w2h[:, h, :], start=(h == 0), stop=False)
                    pe.matmul(rowp[:, t, :], hi, w2l[:, h, :], start=False, stop=False)
                    mm = pe.matmul(rowp[:, t, :], lo, w2h[:, h, :], start=False, stop=False)
                    if h == HC - 1:
                        mm = pe.matmul(rowp[:, t, :], ones3[:], biases[:, 1, :], start=False, stop=True)
                if h == HC - 1:
                    mm.then_inc(fc2_done, 1)

            def rows(m, j, first=False):
                p, l = j // 8, j % 8
                if l == 0 and not (first and j == 0):
                    for h in (6, 7):
                        fc2(m if j else m - 1, 0 if j else 1, h)
                if j == 0:
                    turn_h(m)
                if l == 1:
                    fc(m, p)
                if l == 3:
                    turn_h2(m, p)
                if l == 4:
                    fc1(m, p, 0)
                    fc1(m, p, 1)
                if l >= 5:
                    for h in (2 * l - 10, 2 * l - 9):
                        fc2(m, p, h)
                        fc1(m, p, h + 2)

            def fc1_bias(j):
                pe.wait_ge(w_landed[j % 4], 16 * (j // 4 + 1))
                for i in range(4):
                    h = 4 * (j % 2) + i
                    mm = pe.matmul(rowp[:, 0, h:h + 1], xrows[:, j % 4, P * i:P * i + P], lnc[:, 3, j // 2:j // 2 + 1],
                                   start=(j == 0 and i == 0), stop=(j >= 6), skip_group_check=True)
                mm.then_inc(c1_done, 1)

            for b in range(16):
                attend(0, b)
                if b < 8:
                    fc1_bias(b)
            pe.wait_ge(w_split, 32)
            pe.wait_ge(c1_ready, 1)
            pe.wait_ge(bias_landed, 48)
            for j in range(16):
                attend(1, j)
                rows(0, j, first=True)
            with pe.Fori(2, NB) as n:
                for j in range(16):
                    attend(n, j)
                    rows(n - 1, j)
            for j in range(16):
                rows(NB - 1, j)
            fc2(NB - 1, 1, 6)
            fc2(NB - 1, 1, 7)

        @block.vector
        def _(dve):
            dve.memset(ones3[:], 1.0)
            dve.wait_ge(const_made, 2)
            dve.wait_ge(const_landed, CONSTS)
            prep = Steps(dve, prep_step, 0)
            prep.did(dve.tensor_copy(wx[:, :, 0:F], wraw))
            for i in range(2):
                prep.did(dve.tensor_tensor(wprod, wraw, a_bc[:, F * i:F * i + F].unsqueeze(1).to_broadcast([P, KC, F]),
                                           ALU.mult))
                prep.wait()
                prep.did(dve.tensor_reduce(wx[:, :, F + i:F + i + 1], wprod, AX_X, ALU.add))
                prep.wait()
            for c in range(KC):
                last = dve.tensor_scalar(b1rep[:, c, :], ones[:], lnc[:, 1, c:c + 1], None, ALU.mult)
            prep.did(last)
            dve.wait_ge(prep_sums, 1)
            prep.did(dve.tensor_copy(crow, rowp[:, 0, 0:66]))
            for c in range(KC):
                prep.did(dve.tensor_scalar(wx[:, c, :], wx[:, c, :], lnc[:, 0, c:c + 1], None, ALU.mult))
            bias = Steps(dve, bias_step, 0)
            dve.tensor_copy(fch[:], fcs)
            bias.did(dve.tensor_copy(bparts[:, 0, :, :].rearrange("a v d -> a (v d)"), brow))
            bias.wait()
            dve.tensor_tensor(fcl[:], fcs, fch[:].bitcast(F32), ALU.subtract)
            for t in range(2):
                bias.did(dve.tensor_tensor(brow, brow, bparts[:, t, :, :].rearrange("a v d -> a (v d)"), ALU.subtract))
                bias.wait()
                bias.did(dve.tensor_copy(bparts[:, t + 1, :, :].rearrange("a v d -> a (v d)"), brow))
                bias.wait()

            def stats(b, i, u):
                dve.wait_ge(xin_landed[u], 64 * i + 64)
                for k in range(4):
                    last = dve.bn_stats(stat[:, k, :], xin[u][:, D * k:D * k + D])
                last.then_inc(stats_step, 1)
                dve.wait_ge(stats_step, b + 1)
                dve.sem_inc(aggr_begun, 1)
                for k in range(4):
                    last = dve.bn_aggr(mv[:, u % 2, k, :], stat[:, k, :])
                last.then_inc(stats_done, 1)
                dve.wait_ge(stats_done, b + 1)

            def normalise(b, u):
                dve.wait_ge(rstd_ready, b + 1)
                for k in range(4):
                    xt = xin[u][:, D * k:D * k + D]
                    dve.tensor_scalar(xt, xt, mv[:, u % 2, k, 0:1], rstd[:, u % 2, k:k + 1], ALU.subtract, ALU.mult)\
                       .then_inc(xhat_done, 1)

            def keep_wh(b, u):
                dve.wait_ge(wh_done, b + 1)
                got = rowp[:, u % 2, 0:264].rearrange("p (k f) -> p k f", k=4)
                dve.tensor_tensor(whs[:, bass.ds(4 * b, 4), :], got[:, :, 0:F],
                                  crow[:, 0:F].unsqueeze(1).to_broadcast([P, 4, F]), ALU.add)
                dve.tensor_scalar(s_tab[:, bass.ds(4 * b, 4)], got[:, :, F], crow[:, F:F + 1], None, ALU.add)
                dve.tensor_scalar(nd_tab[:, bass.ds(4 * b, 4)], got[:, :, F + 1], crow[:, F + 1:F + 2], -1.0,
                                  ALU.add, ALU.mult).then_inc(wh_ready, 1)

            stats(0, 0, 0)
            dve.wait_ge(bias_landed, 48)
            for u in range(4):
                stats(u + 1, (u + 1) // 4, (u + 1) % 4)
                normalise(u, u)
                if u:
                    keep_wh(u - 1, u - 1)
            with dve.Fori(1, 3) as i:
                for u in range(4):
                    b = 4 * i + u
                    stats(b + 1, i + (u + 1) // 4, (u + 1) % 4)
                    normalise(b, u)
                    keep_wh(b - 1, (u - 1) % 4)
            for u in range(4):
                b = 12 + u
                if u < 3:
                    stats(b + 1, 3, u + 1)
                normalise(b, u)
                keep_wh(b - 1, (u - 1) % 4)
            keep_wh(15, 3)
            dve.wait_ge(wh_ready, NBL)

            tab = Steps(dve, table_step, 0)
            tab.did(dve.tensor_reduce(dmax[:, 0:1], nd_tab[:], AX_X, ALU.min))
            tab.wait()
            tab.did(dve.tensor_scalar(dmax[:, 0:1], dmax[:, 0:1], -1.0, None, ALU.mult))
            dve.wait_ge(dmax_ready, 1)
            tab.did(dve.tensor_scalar(dmax[:, 2:3], dmax[:, 1:2], -1.0, HEADROOM, ALU.mult, ALU.add))
            tab.did(dve.tensor_scalar(dmax[:, 3:4], dmax[:, 1:2], -SLOPE, HEADROOM, ALU.mult, ALU.add))
            dve.wait_ge(s_turned, 1)
            tab.did(dve.tensor_scalar(t_tab, acc[:, 0, 0:NT], dmax[:, 1:2], None, ALU.add))
            tab.wait()
            tab.did(dve.scalar_tensor_tensor(lt_tab, t_tab, SLOPE, t_tab, ALU.mult, ALU.max))
            tab.wait()
            tab.did(dve.tensor_tensor(ab_tab[:, :, 0], t_tab, lt_tab, ALU.subtract))
            tab.did(dve.scalar_tensor_tensor(ab_tab[:, :, 1], t_tab, SLOPE, lt_tab, ALU.mult, ALU.subtract))
            dve.wait_ge(wsum_done, 1)
            tab.did(dve.tensor_reduce(wsum[:], acc[:, 1, :].rearrange("p (t f) -> p f t", f=F), AX_X, ALU.add))
            dve.wait_ge(exps_done, 1)

            for st in range(STG):
                for t in range(3):
                    for v in range(2):
                        at = 6 * st + 2 * t + v
                        us = u_tab[:, 16 * st:16 * st + 16, v:v + 1]
                        if t == 0:
                            if st:
                                dve.wait_ge(uv_part, at - 1)
                            dve.tensor_copy(uf[v][:, :, F:C1], us)
                            dve.tensor_tensor(uf[v][:, :, 0:F], whs[:, 16 * st:16 * st + 16, :],
                                              us.to_broadcast([P, 16, F]), ALU.mult).then_inc(uv_rest, 1)
                        else:
                            c = PART * v + C1 * (t - 1)
                            dve.wait_ge(uv_part, at - 1)
                            dve.tensor_tensor(uf[v], uf[v], uv[:, 16 * st:16 * st + 16, c:c + C1], ALU.subtract)\
                               .then_inc(uv_rest, 1)
            dve.wait_ge(uv_rest, 6 * STG)

            def turn_piece(n, i):
                st = i // SUB
                dve.wait_ge(bytes_ready, 16 * n + (i + 1))
                if i % SUB == 0 and not (isinstance(n, int) and 16 * n + 4 * st < 8):
                    dve.wait_ge(masks_used, 16 * n + (4 * st - 4))
                g = 4 * (i % SUB)
                dst = edges[:, st % 2, :].rearrange("p (b g r) -> p g b r", b=4, r=Q)[:, g:g + 4, :, :]
                dve.transpose(dst, byte_ring[:, i % BYTES, :].bitcast(U32).rearrange("p (g b w) -> p g b w", g=4, b=4))\
                   .then_inc(turned, 1)

            def masks(n, b):
                at = 48 * n + 3 * b
                if not (isinstance(n, int) and 16 * n + b < CR):
                    dve.wait_ge(masks_used, 16 * n + (b + 1 - CR))
                if b == 0:
                    dve.wait_ge(srow_landed, 16 * n + 16)
                for k in range(4):
                    last = dve.tensor_scalar(sbu[:, b % CR, :, k], srows[:, n % 2, :], nd_tab[:, 4 * b + k:4 * b + k + 1],
                                             float(EDGE_BYTE), ALU.is_lt, ALU.mult)
                last.then_inc(mask_step, 1)
                st = b // 4
                e = edges[:, st % 2, 512 * (b % 4):512 * (b % 4) + 512]
                sg = signs[:, b % CR, :]
                if b % 4 == 0:
                    dve.wait_ge(turned, 16 * n + (4 * st + 4))
                dve.wait_ge(mask_step, at + 1)
                dve.tensor_tensor(sg, e, sg, ALU.bitwise_and).then_inc(mask_step, 1)
                dve.wait_ge(mask_step, at + 2)
                dve.scalar_tensor_tensor(e, e, EDGE_WORD, sg, ALU.bitwise_and, ALU.bitwise_xor).then_inc(mask_step, 1)

            def ahead(n, j, last=False):
                if j % 4 == 2 and not (last and j >= 11):
                    turn_piece(n + (j + 5) // 16, (j + 5) % 16)
                if not (last and j >= 14):
                    masks(n + (j + 2) // 16, (j + 2) % 16)
                for i in {0: (j + 4, j + 5), 1: (j + 5,)}.get(j % 4, ()):
                    if not (last and i >= 16):
                        turn_piece(n + i // 16, i % 16)

            def attention_rows(m):
                ev = Steps(dve, evac_step, EV * m)
                dve.wait_ge(masks_used, 16 * m + 16)
                for s in range(SUB):
                    ev.did(dve.tensor_reduce(red[:, s, :, :], accp[:, s, :, :, :], AX_X, ALU.add))
                ev.wait()
                ab = ab_tab[:, bass.ds(4 * m, 4), :].unsqueeze(3).to_broadcast([P, SUB, 2, C1])
                ev.did(dve.tensor_tensor(red, red, ab, ALU.mult))
                ev.wait()
                ev.did(dve.tensor_tensor(num, red[:, :, 0, :], red[:, :, 1, :], ALU.add))
                ev.wait()
                none, total, inverse = den[:, 0, :], den[:, 1, :], den[:, 2, :]
                ev.did(dve.tensor_scalar(none, num[:, :, F], 0.0, None, ALU.is_equal))
                ev.wait()
                ev.did(dve.scalar_tensor_tensor(total, none, float(N), num[:, :, F], ALU.mult, ALU.add))
                ev.wait()
                ev.did(dve.reciprocal(inverse, total))
                ev.did(dve.tensor_tensor(hp, none.unsqueeze(2).to_broadcast([P, SUB, F]),
                                         wsum[:].unsqueeze(1).to_broadcast([P, SUB, F]), ALU.mult))
                ev.wait()
                ev.did(dve.tensor_tensor(num[:, :, 0:F], num[:, :, 0:F], hp, ALU.add))
                ev.wait()
                ev.did(dve.tensor_tensor(hp, num[:, :, 0:F], inverse.unsqueeze(2).to_broadcast([P, SUB, F]), ALU.mult))
                ev.wait()
                ev.did(dve.tensor_copy(hcat[:, :, 0:F], hp))
                ev.wait()
                ev.did(dve.tensor_tensor(hcat[:, :, F:2 * F], hp, hcat[:, :, 0:F].bitcast(F32), ALU.subtract))

            def add_out(m, p):
                dve.wait_ge(fc2_done, 2 * m + (p + 1))
                xr = xrows[:, 2 * p:2 * p + 2, :]
                dve.tensor_tensor(xr, rowp[:, :, :], xr, ALU.add).then_inc(out_added, 1)

            def add_attention(m, p):
                ln = Steps(dve, ln_step, 2 * LN * m + LN * p)
                dve.wait_ge(fc_done, 2 * m + (p + 1))
                dve.wait_ge(x_landed[p], 16 * m + 16)
                xr = xrows[:, 2 * p:2 * p + 2, :]
                ln.did(dve.tensor_tensor(xr, rowp[:, :, :], xr, ALU.add))
                ln.wait()
                for t in range(2):
                    ln.did(dve.bn_stats(stat[:, t, :], xrows[:, 2 * p + t, :]))
                ln.wait()
                dve.sem_inc(aggr_begun, 1)
                for t in range(2):
                    ln.did(dve.bn_aggr(mv2[:, t, :], stat[:, t, :]))

            def normalise2(m, p):
                ln = Steps(dve, ln_step, 2 * LN * m + (LN * p + 5))
                dve.wait_ge(rstd2_ready, 2 * m + (p + 1))
                for t in range(2):
                    ln.did(dve.tensor_scalar(xhat[:, t, :], xrows[:, 2 * p + t, :], mv2[:, t, 0:1], rstd2[:, t:t + 1],
                                             ALU.subtract, ALU.mult))

            def low_h2(m, p):
                for c in range(2):
                    dve.wait_ge(h2h_ready, 4 * m + (2 * p + c + 1))
                    dve.tensor_tensor(h2l[:, 2 * c:2 * c + 2, :].rearrange("p c i -> p (c i)"), turn[:, c, :],
                                      h2h[:, 2 * c:2 * c + 2, :].rearrange("p c i -> p (c i)").bitcast(F32),
                                      ALU.subtract).then_inc(h2l_ready, 1)

            def low_m(m, p, h):
                dve.wait_ge(gelu_done, 16 * m + (8 * p + h + 1))
                dve.tensor_tensor(m_l[:, h % 2, :], m_f[:, h % 2, :], m_h[:, h % 2, :].bitcast(F32), ALU.subtract)\
                   .then_inc(m_ready, 1)

            def rows(m, j, first=False):
                p, l = j // 8, j % 8
                if l == 0 and not (first and j == 0):
                    add_out(m if j else m - 1, 0 if j else 1)
                if l == 1:
                    add_attention(m, p)
                if l == 2:
                    normalise2(m, p)
                if l == 3:
                    low_h2(m, p)
                if l >= 4:
                    low_m(m, p, 2 * l - 8)
                    low_m(m, p, 2 * l - 7)

            def split_w(j):
                dve.wait_ge(w_landed[j % 4], 16 * (j // 4 + 1))
                src = xrows[:, j % 4, :]
                if j < 8:
                    c, cols = j // 2, slice(512 * (j % 2), 512 * (j % 2) + 512)
                    gain = lnc[:, 2, c:c + 1]
                    dve.tensor_scalar(w1h[:, c, cols], src, gain, None, ALU.mult).then_inc(w_split, 1)
                    dve.wait_ge(w_split, 2 * j + 1)
                    dve.scalar_tensor_tensor(w1l[:, c, cols], src, gain, w1h[:, c, cols].bitcast(F32),
                                             ALU.mult, ALU.subtract).then_inc(w_split, 1)
                else:
                    dve.tensor_copy(w2h[:, j - 8, :], src).then_inc(w_split, 1)
                    dve.wait_ge(w_split, 2 * j + 1)
                    dve.tensor_tensor(w2l[:, j - 8, :], src, w2h[:, j - 8, :].bitcast(F32), ALU.subtract)\
                       .then_inc(w_split, 1)

            for i in range(4):
                turn_piece(0, i)
            masks(0, 0)
            masks(0, 1)
            for j in range(16):
                ahead(0, j)
                split_w(j)
                if j == 8:
                    dve.wait_ge(c1_done, 8)
                    dve.tensor_tensor(c1[:], rowp[:, 0, 0:HC], b1c[:], ALU.add).then_inc(c1_ready, 1)
            dve.wait_ge(exps_done, 2)
            attention_rows(0)
            for j in range(16):
                ahead(1, j)
                rows(0, j, first=True)
            attention_rows(1)
            with dve.Fori(2, NB - 1) as n:
                for j in range(16):
                    ahead(n, j)
                    rows(n - 1, j)
                attention_rows(n)
            for j in range(16):
                ahead(NB - 1, j, last=True)
                rows(NB - 2, j)
            attention_rows(NB - 1)
            for j in range(16):
                rows(NB - 1, j)
            add_out(NB - 1, 1)


_INS = ["x", "adj", "W", "a", "fc_wT", "fc_b", "ln1_g", "ln1_b", "ln2_g", "ln2_b", "fc1_wT", "fc1_b", "fc2_wT", "fc2_b"]


def kernel(x, adj, L0_gnn_W, L0_gnn_a, L0_gnn_fc_w, L0_gnn_fc_b, L0_gnn_ln1_g, L0_gnn_ln1_b, L0_gnn_ln2_g,
           L0_gnn_ln2_b, L0_gnn_fc1_w, L0_gnn_fc1_b, L0_gnn_fc2_w, L0_gnn_fc2_b):
    import numpy as np
    import concourse.bacc as bacc
    from concourse import mybir
    from concourse.bass_utils import run_bass_kernel_spmd

    def columns(v):
        return np.asarray(v).reshape(-1, 128).T

    given = dict(
        x=x, adj=adj, W=L0_gnn_W, a=np.asarray(L0_gnn_a).reshape(1, -1),
        fc_wT=np.asarray(L0_gnn_fc_w).T, fc_b=np.asarray(L0_gnn_fc_b).reshape(1, -1),
        ln1_g=columns(L0_gnn_ln1_g), ln1_b=columns(L0_gnn_ln1_b),
        ln2_g=columns(L0_gnn_ln2_g), ln2_b=columns(L0_gnn_ln2_b),
        fc1_wT=np.asarray(L0_gnn_fc1_w).T, fc1_b=columns(L0_gnn_fc1_b),
        fc2_wT=np.asarray(L0_gnn_fc2_w).T, fc2_b=np.asarray(L0_gnn_fc2_b).reshape(1, -1),
    )
    nc = bacc.Bacc("TRN2", target_bir_lowering=False, num_devices=1)
    arrays, args = {}, []
    for name in _INS:
        v = np.ascontiguousarray(given[name])
        arrays[f"in_{name}"] = v
        args.append(nc.dram_tensor(f"in_{name}", v.shape, mybir.dt.from_np(v.dtype), kind="ExternalInput").ap())
    args.append(nc.dram_tensor("out_rows", arrays["in_x"].shape, mybir.dt.float32, kind="ExternalOutput").ap())
    gat_layer(nc, *args)
    got = run_bass_kernel_spmd(nc, [arrays], core_ids=[0])
    return got.results[0]["out_rows"]
```

```python
from contextlib import ExitStack

import concourse.bass as bass
from concourse import mybir

F32 = mybir.dt.float32
F32R = mybir.dt.float32r
BF16 = mybir.dt.bfloat16
I32 = mybir.dt.int32
I8 = mybir.dt.int8
U8 = mybir.dt.uint8
U32 = mybir.dt.uint32
FP8 = mybir.dt.float8e4
ALU = mybir.AluOpType
ACT = mybir.ActivationFunctionType
AX_X = mybir.AxisListType.X
RMAX = bass.bass_isa.ReduceOp.max

P = 128
Q = 32
SLOPE = 0.2
EPS = 1e-5
HEADROOM = 48.0
EDGE_BYTE = 0x40
EDGE_WORD = 0x40404040


class Steps:

    def __init__(self, eng, sem, before):
        self.eng, self.sem, self.n = eng, sem, before

    def did(self, ins):
        ins.then_inc(self.sem, 1)
        self.n = self.n + 1

    def wait(self):
        self.eng.wait_ge(self.sem, self.n)


def in_register(eng, value):
    return value if isinstance(value, int) else eng.snap(value)


def gat_layer(nc, x, adj, W, a, fc_wT, fc_b, ln1_g, ln1_b, ln2_g, ln2_b, fc1_wT, fc1_b, fc2_wT, fc2_b, out):
    N, D = x.shape
    F = W.shape[1]
    HID = fc1_wT.shape[1]
    KC = D // P
    HC = HID // P
    C1 = F + 1
    PART = 3 * C1
    NB = N // 512
    SUB = 4
    NBL = 16
    STG = 4
    QC = N // 4
    NT = N // P
    RING = 2
    BYTES = 2
    CR = 4
    ACT_K = 2
    EV = 14
    LN = 7
    assert D == 512 and F == 64 and HID == 1024 and N == 8192

    s_dram = nc.dram_tensor("f_src_rows", [1, N], F32).ap()

    with ExitStack() as ctx:
        def sb(name, shape, dt):
            return ctx.enter_context(nc.sbuf_tensor(name, shape, dt))

        def sem(name):
            return ctx.enter_context(nc.semaphore(name))

        uv = sb("uv", [P, NT, 2 * PART], BF16)
        w1h = sb("w1h", [P, KC, HID], F32R)
        w1l = sb("w1l", [P, KC, HID], F32R)
        w2h = sb("w2h", [P, HC, D], F32R)
        w2l = sb("w2l", [P, HC, D], F32R)
        fch = sb("fch", [P, D], F32R)
        fcl = sb("fcl", [P, D], F32R)
        adj_ring = sb("adj_ring", [P, RING, 2048], I32)
        byte_ring = sb("byte_ring", [P, BYTES, 2048], U8)
        edges = sb("edges", [P, 2, 2048], U32)
        signs = sb("signs", [P, CR, 512], U32)
        xrows = sb("xrows", [P, SUB, D], F32)
        work = sb("work", [P, 2080], F32)
        h2h = sb("h2h", [P, KC, 256], F32R)
        h2l = sb("h2l", [P, KC, 256], F32R)
        m_f = sb("m_f", [P, 2, 256], F32)
        m_h = sb("m_h", [P, 2, 256], F32R)
        m_l = sb("m_l", [P, 2, 256], F32R)
        srows = sb("srows", [P, 2, 512], F32)
        hcat = sb("hcat", [P, SUB, P], F32R)
        hT = sb("hT", [P, SUB * P], F32R)
        biases = sb("biases", [3, 2, D], BF16)
        ones3 = sb("ones3", [3, P], BF16)
        ident = sb("ident", [P, P], F32)
        ones = sb("ones", [P, P], F32)
        wsum = sb("wsum", [P, F], F32)
        s_tab = sb("s_tab", [P, NT], F32)
        d_tab = sb("d_tab", [P, NT], F32)
        nd_tab = sb("nd_tab", [P, NT], F32)
        u_tab = sb("u_tab", [P, NT, 2], F32)
        ab_tab = sb("ab_tab", [P, NT, 2], F32)
        c1 = sb("c1", [P, HC], F32)
        b1c = sb("b1c", [P, HC], F32)
        lnc = sb("lnc", [P, 4, KC], F32)
        stat = sb("stat", [P, 4, 6], F32)
        mv = sb("mv", [P, 2, 4, 2], F32)
        rstd = sb("rstd", [P, 2, 4], F32)
        shift = sb("shift", [P, 2, 4], F32)
        mv2 = sb("mv2", [P, 2, 2], F32)
        rstd2 = sb("rstd2", [P, 2], F32)
        mhalf = sb("mhalf", [P, 4], F32)
        eps = sb("eps", [P, 4], F32)
        minus = sb("minus", [P, 4], F32)
        dmax = sb("dmax", [P, 4], F32)
        den = sb("den", [P, 3, SUB], F32)

        acc = ctx.enter_context(nc.psum_tensor("acc", [P, SUB, 512], F32))
        rowp = ctx.enter_context(nc.psum_tensor("rowp", [P, 2, 512], F32))
        turn = ctx.enter_context(nc.psum_tensor("turn", [P, 2, 512], F32))

        whs = edges[:, :, :].bitcast(F32).rearrange("p a b -> p (a b)").rearrange("p (t f) -> p t f", f=F)
        xin = [
            adj_ring[:, 0, :].bitcast(F32), adj_ring[:, 1, :].bitcast(F32),
            xrows[:, :, :].rearrange("p a b -> p (a b)"), work[:, 0:2048],
        ]
        xT = signs[:, :, :].bitcast(F32)
        wx = m_f[:, :, :].rearrange("p a b -> p (a b)")[:, 0:KC * 66].rearrange("p (c f) -> p c f", c=KC)
        wraw = srows[:, 0, 0:KC * F].rearrange("p (c f) -> p c f", c=KC)
        wprod = srows[:, 0, 256:512].rearrange("p (c f) -> p c f", c=KC)
        a_bc = srows[:, 1, 0:2 * F]
        crow = srows[:, 1, 128:194]
        b1rep = xT[:, 3, :].rearrange("p (c m) -> p c m", c=KC)
        snat = m_f[0:NT, 0, 0:P]
        t_tab, lt_tab = m_f[:, 1, 128:128 + NT], m_f[:, 1, 192:192 + NT]
        ef = edges[:, :, :].bitcast(F32)
        brow = ef[0:16, 0, 0:F]
        bparts = edges[:, :, :].bitcast(BF16)[0:16, 1, 0:3 * F].rearrange("q (t c) -> q t c", t=3)
        fcs = ef[:, 1, 1536:2048]

        xhat = work[:, 0:1024].rearrange("p (t d) -> p t d", t=2)
        red = work[:, 1024:1544].rearrange("p (s v c) -> p s v c", s=SUB, v=2)
        num = work[:, 1544:1804].rearrange("p (s c) -> p s c", s=SUB)
        hp = work[:, 1804:2060].rearrange("p (s c) -> p s c", s=SUB)
        uf = [work[:, v * 1040:(v + 1) * 1040].rearrange("p (t c) -> p t c", t=16) for v in range(2)]
        eb = edges[:, :, :].bitcast(FP8).rearrange("p g (b i k) -> p g b i k", b=4, k=4)
        sbm = signs[:, :, :].bitcast(FP8).rearrange("p c (i k) -> p c i k", k=4)
        sbi = signs[:, :, :].bitcast(I8).rearrange("p c (i k) -> p c i k", k=4)
        sbu = signs[:, :, :].bitcast(U8).rearrange("p c (i k) -> p c i k", k=4)
        accp = acc[:, :, 0:2 * PART].rearrange("p s (v t c) -> p s v c t", v=2, t=3)

        const_landed = sem("const_landed")
        late_landed = sem("late_landed")
        const_made = sem("const_made")
        prep_step = sem("prep_step")
        prep_sums = sem("prep_sums")
        xin_landed = [sem(f"xin_landed{i}") for i in range(4)]
        stats_step = sem("stats_step")
        aggr_begun = sem("aggr_begun")
        stats_done = sem("stats_done")
        var_step = sem("var_step")
        exp_table = sem("exp_table")
        rstd_ready = sem("rstd_ready")
        xhat_done = sem("xhat_done")
        xhat_act = sem("xhat_act")
        x_turned = sem("x_turned")
        xT_ready = sem("xT_ready")
        wh_done = sem("wh_done")
        wh_ready = sem("wh_ready")
        table_step = sem("table_step")
        s_stored = sem("s_stored")
        s_landed = sem("s_landed")
        dmax_ready = sem("dmax_ready")
        s_turned = sem("s_turned")
        wsum_done = sem("wsum_done")
        exps_done = sem("exps_done")
        uv_rest = sem("uv_rest")
        uv_part = sem("uv_part")
        srow_landed = sem("srow_landed")
        bias_step = sem("bias_step")
        bias_landed = sem("bias_landed")
        piece_landed = [sem(f"piece_landed{i}") for i in range(RING)]
        bytes_ready = sem("bytes_ready")
        turned = sem("turned")
        act_signs = sem("act_signs")
        signs_begun = sem("signs_begun")
        mask_step = sem("mask_step")
        masks_taken = sem("masks_taken")
        masks_used = sem("masks_used")
        evac_step = sem("evac_step")
        h_turned = sem("h_turned")
        hT_ready = sem("hT_ready")
        fc_done = sem("fc_done")
        ln_step = sem("ln_step")
        var2_step = sem("var2_step")
        rstd2_ready = sem("rstd2_ready")
        h2_turned = sem("h2_turned")
        h2h_ready = sem("h2h_ready")
        h2l_ready = sem("h2l_ready")
        fc1_done = sem("fc1_done")
        gelu_done = sem("gelu_done")
        m_ready = sem("m_ready")
        fc2_done = sem("fc2_done")
        out_added = sem("out_added")
        stored = [sem(f"stored{i}") for i in range(2)]
        x_landed = [sem(f"x_landed{i}") for i in range(2)]
        w_landed = [sem(f"w_landed{i}") for i in range(4)]
        w_high = sem("w_high")
        w_low = sem("w_low")
        c1_done = sem("c1_done")
        c1_ready = sem("c1_ready")

        CONSTS = 16 * 6
        block = ctx.enter_context(nc.Block())

        @block.sync
        def _(sp):
            def load_xin(b, u):
                for q in range(4):
                    sp.dma_start(xin[u][Q * q:Q * q + Q, :],
                                 x[bass.ds(QC * q + P * b, P), :].rearrange("(p k) d -> p (k d)", k=4))\
                      .then_inc(xin_landed[u], 16)

            load_xin(0, 0)
            sp.dma_start(wraw, W.rearrange("(c p) f -> p c f", p=P)).then_inc(const_landed, 16)
            sp.dma_start(a_bc, a.to_broadcast([P, 2 * F])).then_inc(const_landed, 16)
            for i, v in enumerate((ln1_g, ln1_b, ln2_g, ln2_b)):
                sp.dma_start(lnc[:, i, :], v).then_inc(const_landed, 16)
            for u in range(1, 4):
                load_xin(u, u)
            sp.dma_start(b1c[:], fc1_b).then_inc(late_landed, 16)
            sp.dma_start(brow[0:8, :], fc_b).then_inc(late_landed, 16)
            sp.dma_start(brow[8:16, :], fc2_b).then_inc(late_landed, 16)
            for h in range(2):
                sp.dma_start(fcs[F * h:F * h + F, :], fc_wT).then_inc(late_landed, 16)
            sp.wait_ge(bias_step, 5)
            for t in range(3):
                sp.dma_start(biases[t:t + 1, :, :].rearrange("a v (q c) -> a (v q) c", c=F), bparts[:, t, :])\
                  .then_inc(bias_landed, 16)

            with sp.Fori(1, 4) as i:
                for u in range(4):
                    used = in_register(sp, 16 * i + (4 * u - 12))
                    sp.wait_ge(x_turned, used)
                    load_xin(4 * i + u, u)

            sp.wait_ge(wh_ready, NBL)
            for q in range(4):
                sp.dma_start(s_dram[0:1, QC * q:QC * q + QC].rearrange("a (b p k) -> (a p) b k", p=Q, k=4),
                             s_tab[Q * q:Q * q + Q, :].rearrange("p (b k) -> p b k", k=4)).then_inc(s_stored, 16)
            sp.wait_ge(s_stored, 64)
            sp.dma_start(snat, s_dram.rearrange("a (t p) -> (a t) p", p=P)).then_inc(s_landed, 16)

            def load_srows(n):
                sp.dma_start(srows[:, n % 2, :], s_dram[0:1, bass.ds(n * 512, 512)].to_broadcast([P, 512]))\
                  .then_inc(srow_landed, 16)

            load_srows(0)

            def load_piece(n, i):
                for q in range(4):
                    col = QC * q + 512 * (i // SUB)
                    sp.dma_start(adj_ring[Q * q:Q * q + Q, i % RING, :].rearrange("r (g c) -> r g c", g=4),
                                 adj[bass.ds(n * 512 + (i % SUB) * P, P), col:col + 512]
                                 .rearrange("(g r) c -> r g c", r=Q)).then_inc(piece_landed[i % RING], 16)

            for i in range(8):
                if i >= RING:
                    sp.wait_ge(bytes_ready, i - RING + 1)
                load_piece(0, i)

            def load_w(j):
                src = fc1_wT[P * (j // 2):P * (j // 2) + P, 512 * (j % 2):512 * (j % 2) + 512] if j < 8 \
                    else fc2_wT[P * (j - 8):P * (j - 8) + P, :]
                sp.dma_start(xrows[:, j % 4, :], src).then_inc(w_landed[j % 4], 16)

            def load_x(m, p):
                sp.dma_start(xrows[:, 2 * p:2 * p + 2, :],
                             x[bass.ds(m * 512 + p * 256, 256), :].rearrange("(t p) d -> p t d", p=P))\
                  .then_inc(x_landed[p], 16)

            def store(m, p):
                sp.dma_start(out[bass.ds(m * 512 + p * 256, 256), :].rearrange("(t p) d -> p t d", p=P),
                             xrows[:, 2 * p:2 * p + 2, :]).then_inc(stored[p], 16)

            def ahead(n, j, last=False):
                if not (last and j >= 8):
                    due = in_register(sp, 16 * n + (j + 9 - RING))
                    sp.wait_ge(bytes_ready, due)
                    load_piece(n + (j + 8) // 16, (j + 8) % 16)
                if j == 4 and not last:
                    made = in_register(sp, 48 * n + 3)
                    sp.wait_ge(mask_step, made)
                    load_srows(n + 1)

            for j in range(4):
                load_w(j)
            for j in range(16):
                ahead(0, j)
                if 1 <= j < 13:
                    sp.wait_ge(w_low, j)
                    load_w(j + 3)
            sp.wait_ge(w_low, 16)
            load_x(0, 0)
            load_x(0, 1)

            def iteration(n, first=False, last=False):
                m = n - 1
                for j in range(16):
                    ahead(n, j, last)
                    if j == 1 and not first:
                        due = in_register(sp, 2 * n - 2)
                        sp.wait_ge(out_added, due)
                        store(n - 2, 1)
                    if j == 4 and not first:
                        due = in_register(sp, 16 * n - 16)
                        sp.wait_ge(stored[1], due)
                        load_x(n - 1, 1)
                    if j == 9:
                        due = in_register(sp, 2 * n - 1)
                        sp.wait_ge(out_added, due)
                        store(n - 1, 0)
                    if j == 12:
                        due = in_register(sp, 16 * n)
                        sp.wait_ge(stored[0], due)
                        load_x(n, 0)

            iteration(1, first=True)
            with sp.Fori(2, NB - 1) as n:
                iteration(n)
            iteration(NB - 1, last=True)
            sp.wait_ge(out_added, 2 * NB - 2)
            store(NB - 2, 1)
            sp.wait_ge(stored[1], 16 * (NB - 1))
            load_x(NB - 1, 1)
            sp.wait_ge(out_added, 2 * NB - 1)
            store(NB - 1, 0)
            sp.wait_ge(out_added, 2 * NB)
            store(NB - 1, 1)
            for p in range(2):
                sp.wait_ge(stored[p], 16 * NB)

        @block.gpsimd
        def _(pool):
            pool.memset(mhalf[:], -0.5)
            pool.memset(eps[:], EPS)
            pool.memset(minus[:], -1.0)
            pool.memset(ones[:], 1.0).then_inc(const_made, 1)
            pool.wait_ge(const_made, 1)
            pool.affine_select(out=ident[:], in_=ones[:], compare_op=ALU.is_equal, fill=0.0, base=0,
                               pattern=[[-1, P]], channel_multiplier=1).then_inc(const_made, 1)

            def inverse_of(b, s, used):
                pool.wait_ge(stats_done, b + 1)
                if used:
                    pool.wait_ge(xhat_act, 2 * b - 2)
                pool.tensor_tensor(rstd[:, s, :], mv[:, s, :, 1], eps[:], ALU.add)
                pool.tensor_tensor(shift[:, s, :], mv[:, s, :, 0], minus[:], ALU.mult).then_inc(var_step, 1)
                pool.wait_ge(var_step, 2 * b + 1)
                pool.tensor_tensor(rstd[:, s, :], rstd[:, s, :], mhalf[:], ALU.pow).then_inc(var_step, 1)
                pool.wait_ge(var_step, 2 * b + 2)
                pool.tensor_tensor(shift[:, s, :], shift[:, s, :], rstd[:, s, :], ALU.mult).then_inc(rstd_ready, 1)

            for b in range(2):
                inverse_of(b, b, False)
            with pool.Fori(1, NBL // 2) as i:
                for s in range(2):
                    inverse_of(2 * i + s, s, True)

            pool.wait_ge(table_step, 1)
            pool.partition_all_reduce(dmax[:, 1:2], dmax[:, 0:1], P, RMAX).then_inc(dmax_ready, 1)

            for j in range(16):
                pool.wait_ge(w_high, j + 1)
                hi, lo = (w1h, w1l) if j < 8 else (w2h, w2l)
                c, cols = (j // 2, slice(512 * (j % 2), 512 * (j % 2) + 512)) if j < 8 else (j - 8, slice(0, D))
                pool.tensor_tensor(lo[:, c, cols], xrows[:, j % 4, :], hi[:, c, cols].bitcast(F32), ALU.subtract)\
                    .then_inc(w_low, 1)

            with pool.Fori(0, 2 * NB) as g:
                pool.wait_ge(ln_step, LN * g + 5)
                pool.tensor_tensor(rstd2[:], mv2[:, :, 1], eps[:, 0:2], ALU.add).then_inc(var2_step, 1)
                pool.wait_ge(var2_step, g + 1)
                pool.tensor_tensor(rstd2[:], rstd2[:], mhalf[:, 0:2], ALU.pow).then_inc(rstd2_ready, 1)

        @block.scalar
        def _(act):
            act.wait_ge(const_made, 1)
            act.activation(c1[:, 0:4], mhalf[:], ACT.Exp).then_inc(exp_table, 1)

            def move_xT(b, k):
                act.wait_ge(x_turned, 4 * b + (k + 1))
                act.activation(xT[:, k, :], turn[:, k % 2, :], ACT.Copy).then_inc(xT_ready, 1)

            def piece(b, u, first=False):
                act.wait_ge(rstd_ready, b + 1)
                for k in (2, 3):
                    xt = xin[u][:, D * k:D * k + D]
                    act.activation(xt, xt, ACT.Identity, scale=rstd[:, u % 2, k:k + 1], bias=shift[:, u % 2, k:k + 1])\
                       .then_inc(xhat_act, 1)
                if first:
                    act.wait_ge(prep_sums, 1)
                for k in range(4):
                    move_xT(b, k)

            for u in range(4):
                piece(u, u, first=(u == 0))
            with act.Fori(1, 4) as i:
                for u in range(4):
                    piece(4 * i + u, u)

            act.wait_ge(table_step, 4)
            act.activation(u_tab[:, :, 0], d_tab[:], ACT.Exp, bias=dmax[:, 2:3])
            act.activation(u_tab[:, :, 1], d_tab[:], ACT.Exp, scale=SLOPE, bias=dmax[:, 3:4]).then_inc(exps_done, 1)

            def parts(st):
                for t in range(3):
                    for v in range(2):
                        act.wait_ge(uv_rest, 6 * st + 2 * t + v + 1)
                        c = PART * v + C1 * t
                        act.activation(uv[:, 16 * st:16 * st + 16, c:c + C1], uf[v], ACT.Copy).then_inc(uv_part, 1)

            def to_bytes(n, i):
                slot, at = i % RING, i % BYTES
                act.wait_ge(piece_landed[slot], 64 * (8 * n + (i // RING + 1)))
                if not (isinstance(n, int) and n * 16 + i < BYTES):
                    act.wait_ge(turned, 16 * n + (i + 1 - BYTES))
                act.activation(byte_ring[:, at, :].bitcast(I8), adj_ring[:, slot, :], ACT.Sign, scale=-1.0, bias=0.5)\
                   .then_inc(bytes_ready, 1)

            def take_signs(n, b):
                if b == 0:
                    act.wait_ge(srow_landed, 16 * n + 16)
                if not (isinstance(n, int) and 16 * n + b < CR):
                    act.wait_ge(masks_used, 16 * n + (b + 1 - CR))
                    act.sem_inc(signs_begun, 1)
                for k in range(4 - ACT_K, 4):
                    last = act.activation(sbi[:, b % CR, :, k], srows[:, n % 2, :], ACT.Sign,
                                          bias=d_tab[:, 4 * b + k:4 * b + k + 1])
                last.then_inc(act_signs, 1)

            parts(0)
            to_bytes(0, 0)
            parts(1)
            to_bytes(0, 1)
            take_signs(0, 0)
            to_bytes(0, 2)
            to_bytes(0, 3)
            take_signs(0, 1)
            act.wait_ge(table_step, 8)
            act.activation(ab_tab[:], ab_tab[:], ACT.Exp).then_inc(exps_done, 1)
            parts(2)
            parts(3)
            to_bytes(0, 4)
            to_bytes(0, 5)
            take_signs(0, 2)
            act.activation(rstd[:, 0, :], mhalf[:], ACT.Gelu)

            def split_high(j):
                act.wait_ge(w_landed[j % 4], 16 * (j // 4 + 1))
                src = xrows[:, j % 4, :]
                if j < 8:
                    c, cols = j // 2, slice(512 * (j % 2), 512 * (j % 2) + 512)
                    gain = lnc[:, 2, c:c + 1]
                    act.activation(w1h[:, c, cols], src, ACT.Copy, scale=gain)
                    act.wait_ge(c1_done, j + 1)
                    act.activation(src, src, ACT.Copy, scale=gain).then_inc(w_high, 1)
                else:
                    act.activation(w2h[:, j - 8, :], src, ACT.Copy).then_inc(w_high, 1)

            def move_hT(m):
                act.wait_ge(h_turned, m + 1)
                act.activation(hT[:], turn[:, 0, :], ACT.Copy).then_inc(hT_ready, 1)

            def move_h2(m, p):
                for c in range(2):
                    act.wait_ge(h2_turned, 4 * m + (2 * p + c + 1))
                    act.activation(h2h[:, 2 * c:2 * c + 2, :].rearrange("p c i -> p (c i)"), turn[:, c, :], ACT.Copy)\
                       .then_inc(h2h_ready, 1)

            def gelu(m, p, h):
                act.wait_ge(fc1_done, 16 * m + (8 * p + h + 1))
                act.activation(m_f[:, h % 2, :], turn[:, h % 2, 0:256], ACT.Gelu, bias=c1[:, h:h + 1])
                act.activation(m_h[:, h % 2, :], turn[:, h % 2, 0:256], ACT.Gelu, bias=c1[:, h:h + 1])\
                   .then_inc(gelu_done, 1)

            def slot(n, j, m=None, last=False):
                p, l = j // 8, j % 8
                if n is not None and not (last and j >= 13):
                    take_signs(n + (j + 3) // 16, (j + 3) % 16)
                if m is not None:
                    if j == 0:
                        move_hT(m)
                    if l == 3:
                        move_h2(m, p)
                    if l == 4:
                        gelu(m, p, 0)
                if n is not None and not (last and j >= 10):
                    to_bytes(n + (j + 6) // 16, (j + 6) % 16)
                if m is not None and l >= 4:
                    if l > 4:
                        gelu(m, p, 2 * l - 8)
                    gelu(m, p, 2 * l - 7)

            for j in range(16):
                slot(0, j)
                split_high(j)
            act.wait_ge(c1_ready, 1)
            with act.Fori(1, NB - 1) as n:
                for j in range(16):
                    slot(n, j, m=n - 1)
            for j in range(16):
                slot(NB - 1, j, m=NB - 2, last=True)
            for j in range(16):
                slot(None, j, m=NB - 1)

        @block.tensor
        def _(pe):
            pe.wait_ge(prep_step, 6)
            for c in range(KC):
                mm = pe.matmul(rowp[:, 0, 0:66], b1rep[:, c, :], wx[:, c, :], start=(c == 0), stop=(c == KC - 1))
            mm.then_inc(prep_sums, 1)
            pe.wait_ge(prep_step, 11)

            def project_x(b, u, k):
                pe.wait_ge(xT_ready, 4 * b + (k + 1))
                for c in range(KC):
                    mm = pe.matmul(rowp[:, u % 2, 66 * k:66 * k + 66], xT[:, k, P * c:P * c + P], wx[:, c, :],
                                   start=(k == 0 and c == 0), stop=(c == KC - 1), skip_group_check=True)
                if k == 3:
                    mm.then_inc(wh_done, 1)

            def piece(b, u, before):
                for k in range(4):
                    if k < 2:
                        pe.wait_ge(xhat_done, 2 * b + (k + 1))
                    else:
                        pe.wait_ge(xhat_act, 2 * b + (k - 1))
                    for c in range(KC):
                        at = 512 * k + P * c
                        mm = pe.transpose(turn[:, k % 2, P * c:P * c + P], xin[u][:, at:at + P], ident[:])
                    mm.then_inc(x_turned, 1)
                    if k:
                        project_x(b, u, k - 1)
                    elif before:
                        project_x(b - 1, u - 1, 3)
                if before:
                    pe.wait_ge(wh_ready, b)

            piece(0, 0, False)
            for u in range(1, 4):
                piece(u, u, True)
            with pe.Fori(1, 4) as i:
                for u in range(4):
                    piece(4 * i + u, u, True)
            project_x(NBL - 1, 3, 3)

            pe.wait_ge(wh_ready, NBL)
            for g in range(8):
                mm = pe.matmul(turn[:, 1, :], ones[:], whs[:, 8 * g:8 * g + 8, :].rearrange("p t f -> p (t f)"),
                               start=(g == 0), stop=(g == 7))
            mm.then_inc(wsum_done, 1)
            pe.wait_ge(s_landed, 16)
            pe.transpose(turn[:, 0, 0:NT], snat, ident[0:NT, 0:NT]).then_inc(s_turned, 1)

            def attend(n, b):
                if b == 0 and not (isinstance(n, int) and n == 0):
                    pe.wait_ge(evac_step, EV * n + (4 - EV))
                pe.wait_ge(mask_step, 48 * n + (3 * b + 3))
                pe.sem_inc(masks_taken, 1)
                if isinstance(n, int) and n == 0:
                    pe.wait_ge(uv_part, 6 * (b // 4) + 6)
                for s in range(SUB):
                    for k in range(4):
                        c = 4 * b + k
                        pe.matmul(acc[:, s, 0:PART], eb[:, (b // 4) % 2, b % 4, P * s:P * s + P, k], uv[:, c, 0:PART],
                                  start=(c == 0), stop=(c == NT - 1), skip_group_check=True)
                        mm = pe.matmul(acc[:, s, PART:2 * PART], sbm[:, b % CR, P * s:P * s + P, k],
                                       uv[:, c, PART:2 * PART], start=False, stop=(c == NT - 1), skip_group_check=True)
                mm.then_inc(masks_used, 1)

            def turn_h(m):
                pe.wait_ge(evac_step, EV * m + EV)
                for s in range(SUB):
                    mm = pe.transpose(turn[:, 0, P * s:P * s + P], hcat[:, s, :].bitcast(F32), ident[:])
                mm.then_inc(h_turned, 1)

            def fc(m, p):
                pe.wait_ge(hT_ready, m + 1)
                if not (isinstance(m, int) and m == 0 and p == 0):
                    pe.wait_ge(out_added, 2 * m + p)
                for t in range(2):
                    rows = hT[:, P * (2 * p + t):P * (2 * p + t) + P]
                    pe.matmul(rowp[:, t, :], rows, fch[:], start=True, stop=False)
                    pe.matmul(rowp[:, t, :], rows, fcl[:], start=False, stop=False)
                    mm = pe.matmul(rowp[:, t, :], ones3[:], biases[:, 0, :], start=False, stop=True)
                mm.then_inc(fc_done, 1)

            def turn_h2(m, p):
                pe.wait_ge(ln_step, 2 * LN * m + (LN * p + LN))
                for c in range(KC):
                    for t in range(2):
                        at = 256 * (c % 2) + P * t
                        mm = pe.transpose(turn[:, c // 2, at:at + P], xhat[:, t, P * c:P * c + P], ident[:])
                    if c % 2:
                        mm.then_inc(h2_turned, 1)

            def fc1(m, p, h):
                pe.wait_ge(h2l_ready, 4 * m + (2 * p + 2))
                for c in range(KC):
                    w, wl = w1h[:, c, P * h:P * h + P], w1l[:, c, P * h:P * h + P]
                    pe.matmul(turn[:, h % 2, 0:256], w, h2h[:, c, :], start=(c == 0), stop=False)
                    pe.matmul(turn[:, h % 2, 0:256], w, h2l[:, c, :], start=False, stop=False)
                    mm = pe.matmul(turn[:, h % 2, 0:256], wl, h2h[:, c, :], start=False, stop=(c == KC - 1))
                mm.then_inc(fc1_done, 1)

            def fc2(m, p, h):
                pe.wait_ge(m_ready, 16 * m + (8 * p + h + 1))
                for t in range(2):
                    hi, lo = m_h[:, h % 2, P * t:P * t + P], m_l[:, h % 2, P * t:P * t + P]
                    pe.matmul(rowp[:, t, :], hi, w2h[:, h, :], start=(h == 0), stop=False)
                    pe.matmul(rowp[:, t, :], hi, w2l[:, h, :], start=False, stop=False)
                    mm = pe.matmul(rowp[:, t, :], lo, w2h[:, h, :], start=False, stop=False)
                    if h == HC - 1:
                        mm = pe.matmul(rowp[:, t, :], ones3[:], biases[:, 1, :], start=False, stop=True)
                if h == HC - 1:
                    mm.then_inc(fc2_done, 1)

            def rows(m, j, first=False):
                p, l = j // 8, j % 8
                if l == 0 and not (first and j == 0):
                    for h in (6, 7):
                        fc2(m if j else m - 1, 0 if j else 1, h)
                if j == 0:
                    turn_h(m)
                if l == 1:
                    fc(m, p)
                if l == 3:
                    turn_h2(m, p)
                if l == 4:
                    fc1(m, p, 0)
                    fc1(m, p, 1)
                if l >= 5:
                    for h in (2 * l - 10, 2 * l - 9):
                        fc2(m, p, h)
                        fc1(m, p, h + 2)

            def fc1_bias(j):
                pe.wait_ge(w_landed[j % 4], 16 * (j // 4 + 1))
                for i in range(4):
                    h = 4 * (j % 2) + i
                    mm = pe.matmul(rowp[:, 0, h:h + 1], xrows[:, j % 4, P * i:P * i + P], lnc[:, 3, j // 2:j // 2 + 1],
                                   start=(j == 0 and i == 0), stop=(j >= 6), skip_group_check=True)
                mm.then_inc(c1_done, 1)

            for b in range(16):
                attend(0, b)
                if b < 8:
                    fc1_bias(b)
            pe.wait_ge(w_low, 16)
            pe.wait_ge(c1_ready, 1)
            pe.wait_ge(bias_landed, 48)
            for j in range(16):
                attend(1, j)
                rows(0, j, first=True)
            with pe.Fori(2, NB) as n:
                for j in range(16):
                    attend(n, j)
                    rows(n - 1, j)
            for j in range(16):
                rows(NB - 1, j)
            fc2(NB - 1, 1, 6)
            fc2(NB - 1, 1, 7)

        @block.vector
        def _(dve):
            dve.memset(ones3[:], 1.0)

            def stats(b, i, u):
                dve.wait_ge(xin_landed[u], 64 * i + 64)
                for k in range(4):
                    last = dve.bn_stats(stat[:, k, :], xin[u][:, D * k:D * k + D])
                last.then_inc(stats_step, 1)
                dve.wait_ge(stats_step, b + 1)
                dve.sem_inc(aggr_begun, 1)
                for k in range(4):
                    last = dve.bn_aggr(mv[:, u % 2, k, :], stat[:, k, :])
                last.then_inc(stats_done, 1)
                dve.wait_ge(stats_done, b + 1)

            stats(0, 0, 0)
            dve.wait_ge(const_made, 2)
            dve.wait_ge(const_landed, CONSTS)
            prep = Steps(dve, prep_step, 0)
            prep.did(dve.tensor_copy(wx[:, :, 0:F], wraw))
            for i in range(2):
                prep.did(dve.tensor_tensor(wprod, wraw, a_bc[:, F * i:F * i + F].unsqueeze(1).to_broadcast([P, KC, F]),
                                           ALU.mult))
                prep.wait()
                prep.did(dve.tensor_reduce(wx[:, :, F + i:F + i + 1], wprod, AX_X, ALU.add))
                prep.wait()
            for c in range(KC):
                last = dve.tensor_scalar(b1rep[:, c, :], ones[:], lnc[:, 1, c:c + 1], None, ALU.mult)
            prep.did(last)
            dve.wait_ge(prep_sums, 1)
            prep.did(dve.tensor_copy(crow, rowp[:, 0, 0:66]))
            for c in range(KC):
                prep.did(dve.tensor_scalar(wx[:, c, :], wx[:, c, :], lnc[:, 0, c:c + 1], None, ALU.mult))
            def normalise(b, u):
                dve.wait_ge(rstd_ready, b + 1)
                for k in range(2):
                    xt = xin[u][:, D * k:D * k + D]
                    dve.tensor_scalar(xt, xt, mv[:, u % 2, k, 0:1], rstd[:, u % 2, k:k + 1], ALU.subtract, ALU.mult)\
                       .then_inc(xhat_done, 1)

            def keep_wh(b, u):
                dve.wait_ge(wh_done, b + 1)
                got = rowp[:, u % 2, 0:264].rearrange("p (k f) -> p k f", k=4)
                dve.tensor_tensor(whs[:, bass.ds(4 * b, 4), :], got[:, :, 0:F],
                                  crow[:, 0:F].unsqueeze(1).to_broadcast([P, 4, F]), ALU.add)
                dve.tensor_scalar(s_tab[:, bass.ds(4 * b, 4)], got[:, :, F], crow[:, F:F + 1], None, ALU.add)
                dve.tensor_scalar(d_tab[:, bass.ds(4 * b, 4)], got[:, :, F + 1], crow[:, F + 1:F + 2], None,
                                  ALU.add).then_inc(wh_ready, 1)

            def split_small():
                bias = Steps(dve, bias_step, 0)
                dve.wait_ge(late_landed, 16 * 5)
                dve.tensor_copy(fch[:], fcs)
                bias.did(dve.tensor_copy(bparts[:, 0, :], brow))
                bias.wait()
                dve.tensor_tensor(fcl[:], fcs, fch[:].bitcast(F32), ALU.subtract)
                for t in range(2):
                    bias.did(dve.tensor_tensor(brow, brow, bparts[:, t, :], ALU.subtract))
                    bias.wait()
                    bias.did(dve.tensor_copy(bparts[:, t + 1, :], brow))
                    bias.wait()

            for u in range(4):
                stats(u + 1, (u + 1) // 4, (u + 1) % 4)
                normalise(u, u)
                if u == 0:
                    split_small()
                    dve.wait_ge(bias_landed, 48)
                else:
                    keep_wh(u - 1, u - 1)
            with dve.Fori(1, 3) as i:
                for u in range(4):
                    b = 4 * i + u
                    stats(b + 1, i + (u + 1) // 4, (u + 1) % 4)
                    normalise(b, u)
                    keep_wh(b - 1, (u - 1) % 4)
            for u in range(4):
                b = 12 + u
                if u < 3:
                    stats(b + 1, 3, u + 1)
                normalise(b, u)
                keep_wh(b - 1, (u - 1) % 4)
            keep_wh(15, 3)
            dve.wait_ge(wh_ready, NBL)

            tab = Steps(dve, table_step, 0)
            tab.did(dve.tensor_reduce(dmax[:, 0:1], d_tab[:], AX_X, ALU.max))
            tab.did(dve.tensor_scalar(nd_tab[:], d_tab[:], -1.0, None, ALU.mult))
            dve.wait_ge(dmax_ready, 1)
            tab.did(dve.tensor_scalar(dmax[:, 2:3], dmax[:, 1:2], -1.0, HEADROOM, ALU.mult, ALU.add))
            tab.did(dve.tensor_scalar(dmax[:, 3:4], dmax[:, 1:2], -SLOPE, HEADROOM, ALU.mult, ALU.add))

            def uv_rows(st):
                for t in range(3):
                    for v in range(2):
                        at = 6 * st + 2 * t + v
                        us = u_tab[:, 16 * st:16 * st + 16, v:v + 1]
                        if t == 0:
                            if st:
                                dve.wait_ge(uv_part, at - 1)
                            dve.tensor_copy(uf[v][:, :, F:C1], us)
                            dve.tensor_tensor(uf[v][:, :, 0:F], whs[:, 16 * st:16 * st + 16, :],
                                              us.to_broadcast([P, 16, F]), ALU.mult).then_inc(uv_rest, 1)
                        else:
                            c = PART * v + C1 * (t - 1)
                            dve.wait_ge(uv_part, at - 1)
                            dve.tensor_tensor(uf[v], uf[v], uv[:, 16 * st:16 * st + 16, c:c + C1], ALU.subtract)\
                               .then_inc(uv_rest, 1)
                dve.wait_ge(uv_rest, 6 * st + 6)

            def row_tables():
                dve.wait_ge(s_turned, 1)
                tab.did(dve.tensor_scalar(t_tab, turn[:, 0, 0:NT], dmax[:, 1:2], None, ALU.add))
                tab.wait()
                tab.did(dve.scalar_tensor_tensor(lt_tab, t_tab, SLOPE, t_tab, ALU.mult, ALU.max))
                tab.wait()
                tab.did(dve.tensor_tensor(ab_tab[:, :, 0], t_tab, lt_tab, ALU.subtract))
                tab.did(dve.scalar_tensor_tensor(ab_tab[:, :, 1], t_tab, SLOPE, lt_tab, ALU.mult, ALU.subtract))
                tab.did(dve.tensor_reduce(wsum[:], turn[:, 1, :].rearrange("p (t f) -> p f t", f=F), AX_X, ALU.add))

            def turn_piece(n, i):
                st = i // SUB
                dve.wait_ge(bytes_ready, 16 * n + (i + 1))
                if i % SUB == 0 and not (isinstance(n, int) and 16 * n + 4 * st < 8):
                    dve.wait_ge(masks_used, 16 * n + (4 * st - 4))
                g = 4 * (i % SUB)
                dst = edges[:, st % 2, :].rearrange("p (b g r) -> p g b r", b=4, r=Q)[:, g:g + 4, :, :]
                dve.transpose(dst, byte_ring[:, i % BYTES, :].bitcast(U32).rearrange("p (g b w) -> p g b w", g=4, b=4))\
                   .then_inc(turned, 1)

            def own_signs(n, b):
                if not (isinstance(n, int) and 16 * n + b < CR):
                    dve.wait_ge(masks_used, 16 * n + (b + 1 - CR))
                if b == 0:
                    dve.wait_ge(srow_landed, 16 * n + 16)
                for k in range(4 - ACT_K):
                    last = dve.tensor_scalar(sbu[:, b % CR, :, k], srows[:, n % 2, :], nd_tab[:, 4 * b + k:4 * b + k + 1],
                                             float(EDGE_BYTE), ALU.is_lt, ALU.mult)
                last.then_inc(mask_step, 1)

            def masks(n, b, signs_made=False):
                if not signs_made:
                    own_signs(n, b)
                at = 48 * n + 3 * b
                st = b // 4
                e = edges[:, st % 2, 512 * (b % 4):512 * (b % 4) + 512]
                sg = signs[:, b % CR, :]
                if b % 4 == 0:
                    dve.wait_ge(turned, 16 * n + (4 * st + 4))
                dve.wait_ge(act_signs, 16 * n + (b + 1))
                dve.wait_ge(mask_step, at + 1)
                dve.scalar_tensor_tensor(sg, e, EDGE_WORD, sg, ALU.bitwise_and, ALU.bitwise_and).then_inc(mask_step, 1)
                dve.wait_ge(mask_step, at + 2)
                dve.scalar_tensor_tensor(e, e, EDGE_WORD, sg, ALU.bitwise_and, ALU.bitwise_xor).then_inc(mask_step, 1)

            def sum_parts(m):
                ev = Steps(dve, evac_step, EV * m)
                dve.wait_ge(masks_used, 16 * m + 16)
                for s in range(SUB):
                    ev.did(dve.tensor_reduce(red[:, s, :, :], accp[:, s, :, :, :], AX_X, ALU.add))

            def attention_rows(m):
                ev = Steps(dve, evac_step, EV * m + SUB)
                ev.wait()
                ab = ab_tab[:, bass.ds(4 * m, 4), :].unsqueeze(3).to_broadcast([P, SUB, 2, C1])
                ev.did(dve.tensor_tensor(red, red, ab, ALU.mult))
                ev.wait()
                ev.did(dve.tensor_tensor(num, red[:, :, 0, :], red[:, :, 1, :], ALU.add))
                ev.wait()
                none, total, inverse = den[:, 0, :], den[:, 1, :], den[:, 2, :]
                ev.did(dve.tensor_scalar(none, num[:, :, F], 0.0, None, ALU.is_equal))
                ev.wait()
                ev.did(dve.scalar_tensor_tensor(total, none, float(N), num[:, :, F], ALU.mult, ALU.add))
                ev.wait()
                ev.did(dve.reciprocal(inverse, total))
                ev.did(dve.tensor_tensor(hp, none.unsqueeze(2).to_broadcast([P, SUB, F]),
                                         wsum[:].unsqueeze(1).to_broadcast([P, SUB, F]), ALU.mult))
                ev.wait()
                ev.did(dve.tensor_tensor(num[:, :, 0:F], num[:, :, 0:F], hp, ALU.add))
                ev.wait()
                ev.did(dve.tensor_tensor(hp, num[:, :, 0:F], inverse.unsqueeze(2).to_broadcast([P, SUB, F]), ALU.mult))
                ev.wait()
                ev.did(dve.tensor_copy(hcat[:, :, 0:F], hp))
                ev.wait()
                ev.did(dve.tensor_tensor(hcat[:, :, F:2 * F], hp, hcat[:, :, 0:F].bitcast(F32), ALU.subtract))

            def add_out(m, p):
                dve.wait_ge(fc2_done, 2 * m + (p + 1))
                xr = xrows[:, 2 * p:2 * p + 2, :]
                dve.tensor_tensor(xr, rowp[:, :, :], xr, ALU.add).then_inc(out_added, 1)

            def add_attention(m, p):
                ln = Steps(dve, ln_step, 2 * LN * m + LN * p)
                dve.wait_ge(fc_done, 2 * m + (p + 1))
                dve.wait_ge(x_landed[p], 16 * m + 16)
                xr = xrows[:, 2 * p:2 * p + 2, :]
                ln.did(dve.tensor_tensor(xr, rowp[:, :, :], xr, ALU.add))
                ln.wait()
                for t in range(2):
                    ln.did(dve.bn_stats(stat[:, t, :], xrows[:, 2 * p + t, :]))
                ln.wait()
                dve.sem_inc(aggr_begun, 1)
                for t in range(2):
                    ln.did(dve.bn_aggr(mv2[:, t, :], stat[:, t, :]))

            def normalise2(m, p):
                ln = Steps(dve, ln_step, 2 * LN * m + (LN * p + 5))
                dve.wait_ge(rstd2_ready, 2 * m + (p + 1))
                for t in range(2):
                    ln.did(dve.tensor_scalar(xhat[:, t, :], xrows[:, 2 * p + t, :], mv2[:, t, 0:1], rstd2[:, t:t + 1],
                                             ALU.subtract, ALU.mult))

            def low_h2(m, p):
                for c in range(2):
                    dve.wait_ge(h2h_ready, 4 * m + (2 * p + c + 1))
                    dve.tensor_tensor(h2l[:, 2 * c:2 * c + 2, :].rearrange("p c i -> p (c i)"), turn[:, c, :],
                                      h2h[:, 2 * c:2 * c + 2, :].rearrange("p c i -> p (c i)").bitcast(F32),
                                      ALU.subtract).then_inc(h2l_ready, 1)

            def low_m(m, p, h):
                dve.wait_ge(gelu_done, 16 * m + (8 * p + h + 1))
                dve.tensor_tensor(m_l[:, h % 2, :], m_f[:, h % 2, :], m_h[:, h % 2, :].bitcast(F32), ALU.subtract)\
                   .then_inc(m_ready, 1)

            def slot(n, j, m=None, first=False, last=False):
                p, l = j // 8, j % 8

                def turn(*ahead):
                    for i in ahead:
                        if n is not None and not (last and j + i >= 16):
                            turn_piece(n + (j + i) // 16, (j + i) % 16)

                def mask(*ahead):
                    for i in ahead:
                        if n is not None and not (last and j + i >= 16):
                            masks(n + (j + i) // 16, (j + i) % 16)

                if l == 0:
                    if j and m is not None:
                        mask(3)
                        turn(4)
                        add_out(m, 0)
                    else:
                        if m is not None and not first:
                            add_out(m - 1, 1)
                        mask(3)
                        turn(4)
                    turn(5)
                if l == 1:
                    turn(5)
                    if n is not None:
                        own_signs(n, j + 3)
                    if m is not None:
                        add_attention(m, p)
                if l == 2:
                    turn(5)
                    if m is not None:
                        normalise2(m, p)
                    if n is not None:
                        masks(n, j + 2, signs_made=True)
                if l == 3:
                    if m is not None:
                        low_h2(m, p)
                    mask(2)
                if l == 4:
                    turn(4, 5)
                    mask(2)
                    if m is not None:
                        low_m(m, p, 0)
                    mask(3)
                    if m is not None:
                        low_m(m, p, 1)
                if l == 5:
                    turn(5, 6)
                if l >= 5:
                    mask(3)
                if j == 15 and n is not None:
                    sum_parts(n)
                if l >= 5 and m is not None:
                    low_m(m, p, 2 * l - 8)
                    low_m(m, p, 2 * l - 7)

            dve.wait_ge(exps_done, 1)
            uv_rows(0)
            uv_rows(1)
            dve.wait_ge(wsum_done, 1)
            for i in range(4):
                turn_piece(0, i)
            masks(0, 0)
            row_tables()
            masks(0, 1)
            uv_rows(2)
            uv_rows(3)
            masks(0, 2)
            for j in range(16):
                slot(0, j)
                if j == 8:
                    dve.wait_ge(c1_done, 8)
                    dve.tensor_tensor(c1[:], rowp[:, 0, 0:HC], b1c[:], ALU.add).then_inc(c1_ready, 1)
            dve.wait_ge(exps_done, 2)
            attention_rows(0)
            for j in range(16):
                slot(1, j, m=0, first=True)
            attention_rows(1)
            with dve.Fori(2, NB - 1) as n:
                for j in range(16):
                    slot(n, j, m=n - 1)
                attention_rows(n)
            for j in range(16):
                slot(NB - 1, j, m=NB - 2, last=True)
            attention_rows(NB - 1)
            for j in range(16):
                slot(None, j, m=NB - 1)
            add_out(NB - 1, 1)


_INS = ["x", "adj", "W", "a", "fc_wT", "fc_b", "ln1_g", "ln1_b", "ln2_g", "ln2_b", "fc1_wT", "fc1_b", "fc2_wT", "fc2_b"]


def kernel(x, adj, L0_gnn_W, L0_gnn_a, L0_gnn_fc_w, L0_gnn_fc_b, L0_gnn_ln1_g, L0_gnn_ln1_b, L0_gnn_ln2_g,
           L0_gnn_ln2_b, L0_gnn_fc1_w, L0_gnn_fc1_b, L0_gnn_fc2_w, L0_gnn_fc2_b):
    import numpy as np
    import concourse.bacc as bacc
    from concourse import mybir
    from concourse.bass_utils import run_bass_kernel_spmd

    def columns(v):
        return np.asarray(v).reshape(-1, 128).T

    given = dict(
        x=x, adj=adj, W=L0_gnn_W, a=np.asarray(L0_gnn_a).reshape(1, -1),
        fc_wT=np.asarray(L0_gnn_fc_w).T, fc_b=np.asarray(L0_gnn_fc_b).reshape(8, -1),
        ln1_g=columns(L0_gnn_ln1_g), ln1_b=columns(L0_gnn_ln1_b),
        ln2_g=columns(L0_gnn_ln2_g), ln2_b=columns(L0_gnn_ln2_b),
        fc1_wT=np.asarray(L0_gnn_fc1_w).T, fc1_b=columns(L0_gnn_fc1_b),
        fc2_wT=np.asarray(L0_gnn_fc2_w).T, fc2_b=np.asarray(L0_gnn_fc2_b).reshape(8, -1),
    )
    nc = bacc.Bacc("TRN2", target_bir_lowering=False, num_devices=1)
    arrays, args = {}, []
    for name in _INS:
        v = np.ascontiguousarray(given[name])
        arrays[f"in_{name}"] = v
        args.append(nc.dram_tensor(f"in_{name}", v.shape, mybir.dt.from_np(v.dtype), kind="ExternalInput").ap())
    args.append(nc.dram_tensor("out_rows", arrays["in_x"].shape, mybir.dt.float32, kind="ExternalOutput").ap())
    gat_layer(nc, *args)
    got = run_bass_kernel_spmd(nc, [arrays], core_ids=[0])
    return got.results[0]["out_rows"]
```

```python
from contextlib import ExitStack

import concourse.bass as bass
from concourse import mybir

F32 = mybir.dt.float32
F32R = mybir.dt.float32r
BF16 = mybir.dt.bfloat16
I32 = mybir.dt.int32
I8 = mybir.dt.int8
U8 = mybir.dt.uint8
U32 = mybir.dt.uint32
FP8 = mybir.dt.float8e4
ALU = mybir.AluOpType
ACT = mybir.ActivationFunctionType
AX_X = mybir.AxisListType.X
RMAX = bass.bass_isa.ReduceOp.max

P = 128
Q = 32
SLOPE = 0.2
EPS = 1e-5
HEADROOM = 48.0
EDGE_BYTE = 0x40
EDGE_WORD = 0x40404040


class Steps:

    def __init__(self, eng, sem, before):
        self.eng, self.sem, self.n = eng, sem, before

    def did(self, ins):
        ins.then_inc(self.sem, 1)
        self.n = self.n + 1

    def wait(self):
        self.eng.wait_ge(self.sem, self.n)


def in_register(eng, value):
    return value if isinstance(value, int) else eng.snap(value)


def gat_layer(nc, x, adj, W, a, fc_wT, fc_b, ln1_g, ln1_b, ln2_g, ln2_b, fc1_wT, fc1_b, fc2_wT, fc2_b, out):
    N, D = x.shape
    F = W.shape[1]
    HID = fc1_wT.shape[1]
    KC = D // P
    HC = HID // P
    C1 = F + 1
    PART = 3 * C1
    NB = N // 512
    SUB = 4
    NBL = 16
    STG = 4
    QC = N // 4
    NT = N // P
    RING = 2
    BYTES = 2
    CR = 4

    def w_chunks(j):
        return range(j, j + 1) if j < 12 else range(2 * j - 12, min(2 * j - 10, 16))

    def act_chunks(n, b):
        return range(3 if isinstance(n, int) and n == 0 else 1 if b in (3, 4, 5) else 2, 4)

    EV = 14
    LN = 7
    assert D == 512 and F == 64 and HID == 1024 and N == 8192

    s_dram = nc.dram_tensor("f_src_rows", [1, N], F32).ap()

    with ExitStack() as ctx:
        def sb(name, shape, dt):
            return ctx.enter_context(nc.sbuf_tensor(name, shape, dt))

        def sem(name):
            return ctx.enter_context(nc.semaphore(name))

        uv = sb("uv", [P, NT, 2 * PART], BF16)
        w1h = sb("w1h", [P, KC, HID], F32R)
        w1l = sb("w1l", [P, KC, HID], F32R)
        w2h = sb("w2h", [P, HC, D], F32R)
        w2l = sb("w2l", [P, HC, D], F32R)
        fch = sb("fch", [P, D], F32R)
        fcl = sb("fcl", [P, D], F32R)
        adj_ring = sb("adj_ring", [P, RING, 2048], I32)
        byte_ring = sb("byte_ring", [P, BYTES, 2048], U8)
        edges = sb("edges", [P, 2, 2048], U32)
        signs = sb("signs", [P, CR, 512], U32)
        xrows = sb("xrows", [P, SUB, D], F32)
        work = sb("work", [P, 2080], F32)
        h2h = sb("h2h", [P, KC, 256], F32R)
        h2l = sb("h2l", [P, KC, 256], F32R)
        m_f = sb("m_f", [P, 2, 256], F32)
        m_h = sb("m_h", [P, 2, 256], F32R)
        m_l = sb("m_l", [P, 2, 256], F32R)
        srows = sb("srows", [P, 2, 512], F32)
        hcat = sb("hcat", [P, SUB, P], F32R)
        hT = sb("hT", [P, SUB * P], F32R)
        biases = sb("biases", [P, 2, D], F32)
        ident = sb("ident", [P, P], F32)
        ones = sb("ones", [P, P], F32)
        wsum = sb("wsum", [P, F], F32)
        s_tab = sb("s_tab", [P, NT], F32)
        d_tab = sb("d_tab", [P, NT], F32)
        nd_tab = sb("nd_tab", [P, NT], F32)
        u_tab = sb("u_tab", [P, NT, 2], F32)
        ab_tab = sb("ab_tab", [P, NT, 2], F32)
        c1 = sb("c1", [P, HC], F32)
        b1c = sb("b1c", [P, HC], F32)
        lnc = sb("lnc", [P, 4, KC], F32)
        stat = sb("stat", [P, 4, 6], F32)
        mv = sb("mv", [P, 2, 4, 2], F32)
        rstd = sb("rstd", [P, 2, 4], F32)
        shift = sb("shift", [P, 2, 4], F32)
        mv2 = sb("mv2", [P, 2, 2], F32)
        rstd2 = sb("rstd2", [P, 2], F32)
        mhalf = sb("mhalf", [P, 4], F32)
        eps = sb("eps", [P, 4], F32)
        minus = sb("minus", [P, 4], F32)
        dmax = sb("dmax", [P, 4], F32)
        den = sb("den", [P, 3, SUB], F32)

        acc = ctx.enter_context(nc.psum_tensor("acc", [P, SUB, 512], F32))
        rowp = ctx.enter_context(nc.psum_tensor("rowp", [P, 2, 512], F32))
        turn = ctx.enter_context(nc.psum_tensor("turn", [P, 2, 512], F32))

        whs = edges[:, :, :].bitcast(F32).rearrange("p a b -> p (a b)").rearrange("p (t f) -> p t f", f=F)
        xin = [
            adj_ring[:, 0, :].bitcast(F32), adj_ring[:, 1, :].bitcast(F32),
            xrows[:, :, :].rearrange("p a b -> p (a b)"), work[:, 0:2048],
        ]
        xT = signs[:, :, :].bitcast(F32)
        wx = m_f[:, :, :].rearrange("p a b -> p (a b)")[:, 0:KC * 66].rearrange("p (c f) -> p c f", c=KC)
        wraw = srows[:, 0, 0:KC * F].rearrange("p (c f) -> p c f", c=KC)
        wprod = srows[:, 0, 256:512].rearrange("p (c f) -> p c f", c=KC)
        a_bc = srows[:, 1, 0:2 * F]
        crow = srows[:, 1, 128:194]
        b1rep = xT[:, 3, :].rearrange("p (c m) -> p c m", c=KC)
        snat = m_f[0:NT, 0, 0:P]
        t_tab, lt_tab = m_f[:, 1, 128:128 + NT], m_f[:, 1, 192:192 + NT]
        ef = edges[:, :, :].bitcast(F32)
        fcs = ef[:, 1, 1536:2048]

        xhat = work[:, 0:1024].rearrange("p (t d) -> p t d", t=2)
        red = work[:, 1024:1544].rearrange("p (s v c) -> p s v c", s=SUB, v=2)
        num = work[:, 1544:1804].rearrange("p (s c) -> p s c", s=SUB)
        hp = work[:, 1804:2060].rearrange("p (s c) -> p s c", s=SUB)
        uf = [work[:, v * 1040:(v + 1) * 1040].rearrange("p (t c) -> p t c", t=16) for v in range(2)]
        eb = edges[:, :, :].bitcast(FP8).rearrange("p g (b i k) -> p g b i k", b=4, k=4)
        sbm = signs[:, :, :].bitcast(FP8).rearrange("p c (i k) -> p c i k", k=4)
        sbi = signs[:, :, :].bitcast(I8).rearrange("p c (i k) -> p c i k", k=4)
        sbu = signs[:, :, :].bitcast(U8).rearrange("p c (i k) -> p c i k", k=4)
        accp = acc[:, :, 0:2 * PART].rearrange("p s (v t c) -> p s v c t", v=2, t=3)

        const_landed = sem("const_landed")
        late_landed = sem("late_landed")
        const_made = sem("const_made")
        prep_step = sem("prep_step")
        prep_sums = sem("prep_sums")
        xin_landed = [sem(f"xin_landed{i}") for i in range(4)]
        stats_step = sem("stats_step")
        aggr_begun = sem("aggr_begun")
        stats_done = sem("stats_done")
        var_step = sem("var_step")
        exp_table = sem("exp_table")
        rstd_ready = sem("rstd_ready")
        xhat_done = sem("xhat_done")
        xhat_act = sem("xhat_act")
        x_turned = sem("x_turned")
        xT_ready = sem("xT_ready")
        wh_done = sem("wh_done")
        wh_ready = sem("wh_ready")
        table_step = sem("table_step")
        s_stored = sem("s_stored")
        s_landed = sem("s_landed")
        dmax_ready = sem("dmax_ready")
        s_turned = sem("s_turned")
        wsum_done = sem("wsum_done")
        exps_done = sem("exps_done")
        uv_rest = sem("uv_rest")
        uv_part = sem("uv_part")
        srow_landed = sem("srow_landed")
        fc_high = sem("fc_high")
        x_biased = sem("x_biased")
        out_biased = sem("out_biased")
        piece_landed = [sem(f"piece_landed{i}") for i in range(RING)]
        bytes_ready = sem("bytes_ready")
        turned = sem("turned")
        act_signs = sem("act_signs")
        signs_begun = sem("signs_begun")
        mask_step = sem("mask_step")
        masks_taken = sem("masks_taken")
        masks_used = sem("masks_used")
        evac_step = sem("evac_step")
        h_turned = sem("h_turned")
        hT_ready = sem("hT_ready")
        fc_done = sem("fc_done")
        ln_step = sem("ln_step")
        var2_step = sem("var2_step")
        rstd2_ready = sem("rstd2_ready")
        h2_turned = sem("h2_turned")
        h2h_ready = sem("h2h_ready")
        h2l_ready = sem("h2l_ready")
        fc1_done = sem("fc1_done")
        gelu_done = sem("gelu_done")
        m_ready = sem("m_ready")
        fc2_done = sem("fc2_done")
        out_added = sem("out_added")
        stored = [sem(f"stored{i}") for i in range(2)]
        x_landed = [sem(f"x_landed{i}") for i in range(2)]
        w_landed = [sem(f"w_landed{i}") for i in range(4)]
        w_scaled = sem("w_scaled")
        w_high = sem("w_high")
        w_low = sem("w_low")
        c1_done = sem("c1_done")
        c1_ready = sem("c1_ready")

        CONSTS = 16 * 6
        block = ctx.enter_context(nc.Block())

        @block.sync
        def _(sp):
            def load_xin(b, u):
                for q in range(4):
                    sp.dma_start(xin[u][Q * q:Q * q + Q, :],
                                 x[bass.ds(QC * q + P * b, P), :].rearrange("(p k) d -> p (k d)", k=4))\
                      .then_inc(xin_landed[u], 16)

            load_xin(0, 0)
            sp.dma_start(wraw, W.rearrange("(c p) f -> p c f", p=P)).then_inc(const_landed, 16)
            sp.dma_start(a_bc, a.to_broadcast([P, 2 * F])).then_inc(const_landed, 16)
            for i, v in enumerate((ln1_g, ln1_b, ln2_g, ln2_b)):
                sp.dma_start(lnc[:, i, :], v).then_inc(const_landed, 16)
            for u in range(1, 4):
                load_xin(u, u)
            sp.dma_start(b1c[:], fc1_b).then_inc(late_landed, 16)
            for i, v in enumerate((fc_b, fc2_b)):
                sp.dma_start(biases[:, i, :], v.to_broadcast([P, D])).then_inc(late_landed, 16)
            for h in range(2):
                sp.dma_start(fcs[F * h:F * h + F, :], fc_wT).then_inc(late_landed, 16)
            with sp.Fori(1, 4) as i:
                for u in range(4):
                    used = in_register(sp, 16 * i + (4 * u - 12))
                    sp.wait_ge(x_turned, used)
                    load_xin(4 * i + u, u)

            sp.wait_ge(wh_ready, NBL)
            for q in range(4):
                sp.dma_start(s_dram[0:1, QC * q:QC * q + QC].rearrange("a (b p k) -> (a p) b k", p=Q, k=4),
                             s_tab[Q * q:Q * q + Q, :].rearrange("p (b k) -> p b k", k=4)).then_inc(s_stored, 16)
            sp.wait_ge(s_stored, 64)
            sp.dma_start(snat, s_dram.rearrange("a (t p) -> (a t) p", p=P)).then_inc(s_landed, 16)

            def load_srows(n):
                sp.dma_start(srows[:, n % 2, :], s_dram[0:1, bass.ds(n * 512, 512)].to_broadcast([P, 512]))\
                  .then_inc(srow_landed, 16)

            load_srows(0)

            def load_piece(n, i):
                for q in range(4):
                    col = QC * q + 512 * (i // SUB)
                    sp.dma_start(adj_ring[Q * q:Q * q + Q, i % RING, :].rearrange("r (g c) -> r g c", g=4),
                                 adj[bass.ds(n * 512 + (i % SUB) * P, P), col:col + 512]
                                 .rearrange("(g r) c -> r g c", r=Q)).then_inc(piece_landed[i % RING], 16)

            def load_w(j):
                src = fc1_wT[P * (j // 2):P * (j // 2) + P, 512 * (j % 2):512 * (j % 2) + 512] if j < 8 \
                    else fc2_wT[P * (j - 8):P * (j - 8) + P, :]
                sp.dma_start(xrows[:, j % 4, :], src).then_inc(w_landed[j % 4], 16)

            for i in range(8):
                if i >= RING:
                    sp.wait_ge(bytes_ready, i - RING + 1)
                load_piece(0, i)
                if i == 1:
                    for j in range(4):
                        load_w(j)

            def load_x(m, p):
                sp.dma_start(xrows[:, 2 * p:2 * p + 2, :],
                             x[bass.ds(m * 512 + p * 256, 256), :].rearrange("(t p) d -> p t d", p=P))\
                  .then_inc(x_landed[p], 16)

            def store(m, p):
                sp.dma_start(out[bass.ds(m * 512 + p * 256, 256), :].rearrange("(t p) d -> p t d", p=P),
                             xrows[:, 2 * p:2 * p + 2, :]).then_inc(stored[p], 16)

            def ahead(n, j, last=False):
                if not (last and j >= 8):
                    due = in_register(sp, 16 * n + (j + 9 - RING))
                    sp.wait_ge(bytes_ready, due)
                    load_piece(n + (j + 8) // 16, (j + 8) % 16)
                if j == 4 and not last:
                    made = in_register(sp, 48 * n + 3)
                    sp.wait_ge(mask_step, made)
                    load_srows(n + 1)

            for j in range(16):
                ahead(0, j)
                for c in w_chunks(j - 1) if j else ():
                    if c < 12:
                        sp.wait_ge(w_low, c + 1)
                        load_w(c + 4)
            sp.wait_ge(w_low, 16)
            load_x(0, 0)
            load_x(0, 1)

            def iteration(n, first=False, last=False):
                m = n - 1
                for j in range(16):
                    ahead(n, j, last)
                    if j == 1 and not first:
                        due = in_register(sp, 2 * n - 2)
                        sp.wait_ge(out_added, due)
                        store(n - 2, 1)
                    if j == 4 and not first:
                        due = in_register(sp, 16 * n - 16)
                        sp.wait_ge(stored[1], due)
                        load_x(n - 1, 1)
                    if j == 9:
                        due = in_register(sp, 2 * n - 1)
                        sp.wait_ge(out_added, due)
                        store(n - 1, 0)
                    if j == 12:
                        due = in_register(sp, 16 * n)
                        sp.wait_ge(stored[0], due)
                        load_x(n, 0)

            iteration(1, first=True)
            with sp.Fori(2, NB - 1) as n:
                iteration(n)
            iteration(NB - 1, last=True)
            sp.wait_ge(out_added, 2 * NB - 2)
            store(NB - 2, 1)
            sp.wait_ge(stored[1], 16 * (NB - 1))
            load_x(NB - 1, 1)
            sp.wait_ge(out_added, 2 * NB - 1)
            store(NB - 1, 0)
            sp.wait_ge(out_added, 2 * NB)
            store(NB - 1, 1)
            for p in range(2):
                sp.wait_ge(stored[p], 16 * NB)

        @block.gpsimd
        def _(pool):
            pool.memset(mhalf[:], -0.5)
            pool.memset(eps[:], EPS)
            pool.memset(minus[:], -1.0)
            pool.memset(ones[:], 1.0).then_inc(const_made, 1)
            pool.wait_ge(const_made, 1)
            pool.affine_select(out=ident[:], in_=ones[:], compare_op=ALU.is_equal, fill=0.0, base=0,
                               pattern=[[-1, P]], channel_multiplier=1).then_inc(const_made, 1)

            def inverse_of(b, s, used):
                pool.wait_ge(stats_done, b + 1)
                if used:
                    pool.wait_ge(xhat_act, 2 * b - 2)
                pool.tensor_tensor(rstd[:, s, :], mv[:, s, :, 1], eps[:], ALU.add)
                pool.tensor_tensor(shift[:, s, :], mv[:, s, :, 0], minus[:], ALU.mult).then_inc(var_step, 1)
                pool.wait_ge(var_step, 2 * b + 1)
                pool.tensor_tensor(rstd[:, s, :], rstd[:, s, :], mhalf[:], ALU.pow).then_inc(var_step, 1)
                pool.wait_ge(var_step, 2 * b + 2)
                pool.tensor_tensor(shift[:, s, :], shift[:, s, :], rstd[:, s, :], ALU.mult).then_inc(rstd_ready, 1)

            for b in range(2):
                inverse_of(b, b, False)
            with pool.Fori(1, NBL // 2) as i:
                for s in range(2):
                    inverse_of(2 * i + s, s, True)

            pool.wait_ge(table_step, 1)
            pool.partition_all_reduce(dmax[:, 1:2], dmax[:, 0:1], P, RMAX).then_inc(dmax_ready, 1)

            def scale_w(j):
                pool.wait_ge(c1_done, j + 1)
                pool.tensor_tensor(xrows[:, j % 4, :], xrows[:, j % 4, :],
                                   lnc[:, 2, j // 2:j // 2 + 1].to_broadcast([P, D]), ALU.mult).then_inc(w_scaled, 1)

            scale_w(0)
            for j in range(16):
                if j < 7:
                    scale_w(j + 1)
                pool.wait_ge(w_high, j + 1)
                hi, lo = (w1h, w1l) if j < 8 else (w2h, w2l)
                c, cols = (j // 2, slice(512 * (j % 2), 512 * (j % 2) + 512)) if j < 8 else (j - 8, slice(0, D))
                pool.tensor_tensor(lo[:, c, cols], xrows[:, j % 4, :], hi[:, c, cols].bitcast(F32), ALU.subtract)\
                    .then_inc(w_low, 1)

            def bias_x(m, p):
                pool.wait_ge(x_landed[p], 16 * m + 16)
                xr = xrows[:, 2 * p:2 * p + 2, :]
                pool.tensor_tensor(xr, xr, biases[:, 0:1, :].to_broadcast([P, 2, D]), ALU.add).then_inc(x_biased, 1)

            def layer_norm(m, p):
                pool.wait_ge(ln_step, 2 * LN * m + (LN * p + 5))
                pool.tensor_tensor(rstd2[:], mv2[:, :, 1], eps[:, 0:2], ALU.add).then_inc(var2_step, 1)
                pool.wait_ge(var2_step, 2 * m + (p + 1))
                pool.tensor_tensor(rstd2[:], rstd2[:], mhalf[:, 0:2], ALU.pow).then_inc(rstd2_ready, 1)
                pool.wait_ge(ln_step, 2 * LN * m + (LN * p + LN))
                xr = xrows[:, 2 * p:2 * p + 2, :]
                pool.tensor_tensor(xr, xr, biases[:, 1:2, :].to_broadcast([P, 2, D]), ALU.add).then_inc(out_biased, 1)

            pool.wait_ge(late_landed, 16 * 5)
            bias_x(0, 0)
            with pool.Fori(0, NB - 1) as m:
                layer_norm(m, 0)
                bias_x(m, 1)
                layer_norm(m, 1)
                bias_x(m + 1, 0)
            layer_norm(NB - 1, 0)
            bias_x(NB - 1, 1)
            layer_norm(NB - 1, 1)

        @block.scalar
        def _(act):
            act.wait_ge(const_made, 1)
            act.activation(c1[:, 0:4], mhalf[:], ACT.Exp).then_inc(exp_table, 1)

            def move_xT(b, k):
                act.wait_ge(x_turned, 4 * b + (k + 1))
                act.activation(xT[:, k, :], turn[:, k % 2, :], ACT.Copy).then_inc(xT_ready, 1)

            def piece(b, u, first=False):
                act.wait_ge(rstd_ready, b + 1)
                for k in (2, 3):
                    xt = xin[u][:, D * k:D * k + D]
                    act.activation(xt, xt, ACT.Identity, scale=rstd[:, u % 2, k:k + 1], bias=shift[:, u % 2, k:k + 1])\
                       .then_inc(xhat_act, 1)
                if first:
                    act.wait_ge(prep_sums, 1)
                for k in range(4):
                    move_xT(b, k)

            for u in range(4):
                piece(u, u, first=(u == 0))
            with act.Fori(1, 4) as i:
                for u in range(4):
                    piece(4 * i + u, u)

            act.wait_ge(table_step, 4)
            act.activation(u_tab[:, :, 0], d_tab[:], ACT.Exp, bias=dmax[:, 2:3])
            act.activation(u_tab[:, :, 1], d_tab[:], ACT.Exp, scale=SLOPE, bias=dmax[:, 3:4]).then_inc(exps_done, 1)

            def parts(st):
                for t in range(2):
                    for v in range(2):
                        act.wait_ge(uv_rest, 6 * st + 2 * t + v + 1)
                        c = PART * v + C1 * t
                        act.activation(uv[:, 16 * st:16 * st + 16, c:c + C1], uf[v], ACT.Copy).then_inc(uv_part, 1)

            def to_bytes(n, i):
                slot, at = i % RING, i % BYTES
                act.wait_ge(piece_landed[slot], 64 * (8 * n + (i // RING + 1)))
                if not (isinstance(n, int) and n * 16 + i < BYTES):
                    act.wait_ge(turned, 16 * n + (i + 1 - BYTES))
                act.activation(byte_ring[:, at, :].bitcast(I8), adj_ring[:, slot, :], ACT.Sign, scale=-1.0, bias=0.5)\
                   .then_inc(bytes_ready, 1)

            def take_signs(n, b):
                if b == 0:
                    act.wait_ge(srow_landed, 16 * n + 16)
                if not (isinstance(n, int) and 16 * n + b < CR):
                    act.wait_ge(masks_used, 16 * n + (b + 1 - CR))
                    act.sem_inc(signs_begun, 1)
                for k in act_chunks(n, b):
                    last = act.activation(sbi[:, b % CR, :, k], srows[:, n % 2, :], ACT.Sign,
                                          bias=d_tab[:, 4 * b + k:4 * b + k + 1])
                last.then_inc(act_signs, 1)

            parts(0)
            parts(1)
            to_bytes(0, 0)
            to_bytes(0, 1)
            parts(2)
            to_bytes(0, 2)
            to_bytes(0, 3)
            take_signs(0, 0)
            take_signs(0, 1)
            act.wait_ge(table_step, 8)
            act.activation(ab_tab[:], ab_tab[:], ACT.Exp).then_inc(exps_done, 1)
            take_signs(0, 2)
            act.activation(rstd[:, 0, :], mhalf[:], ACT.Gelu)
            to_bytes(0, 4)
            to_bytes(0, 5)
            parts(3)

            def split_high(j):
                if j < 8:
                    act.wait_ge(w_scaled, j + 1)
                    high = w1h[:, j // 2, 512 * (j % 2):512 * (j % 2) + 512]
                else:
                    act.wait_ge(w_landed[j % 4], 16 * (j // 4 + 1))
                    high = w2h[:, j - 8, :]
                act.activation(high, xrows[:, j % 4, :], ACT.Copy).then_inc(w_high, 1)

            def move_hT(m):
                act.wait_ge(h_turned, m + 1)
                act.activation(hT[:], turn[:, 0, :], ACT.Copy).then_inc(hT_ready, 1)

            def move_h2(m, p, of=turn):
                for c in range(2):
                    act.wait_ge(h2_turned, 4 * m + (2 * p + c + 1))
                    act.activation(h2h[:, 2 * c:2 * c + 2, :].rearrange("p c i -> p (c i)"), of[:, c, :], ACT.Copy)\
                       .then_inc(h2h_ready, 1)

            def gelu(m, p, h):
                act.wait_ge(fc1_done, 16 * m + (8 * p + h + 1))
                act.activation(m_f[:, h % 2, :], turn[:, h % 2, 0:256], ACT.Gelu, bias=c1[:, h:h + 1])
                act.activation(m_h[:, h % 2, :], turn[:, h % 2, 0:256], ACT.Gelu, bias=c1[:, h:h + 1])\
                   .then_inc(gelu_done, 1)

            def slot(n, j, m=None, last=False):
                p, l = j // 8, j % 8
                if n is not None and not (last and j >= 13):
                    take_signs(n + (j + 3) // 16, (j + 3) % 16)
                if m is not None:
                    if j == 0:
                        move_hT(m)
                    if l == 3:
                        move_h2(m, p)
                    if l == 4:
                        gelu(m, p, 0)
                if n is not None and not (last and j >= 10):
                    to_bytes(n + (j + 6) // 16, (j + 6) % 16)
                if m is not None and l >= 4:
                    if l > 4:
                        gelu(m, p, 2 * l - 8)
                    gelu(m, p, 2 * l - 7)

            for j in range(16):
                slot(0, j)
                for c in w_chunks(j):
                    split_high(c)
            act.wait_ge(c1_ready, 1)
            with act.Fori(1, NB - 1) as n:
                for j in range(16):
                    slot(n, j, m=n - 1)
            for j in range(16):
                slot(NB - 1, j, m=NB - 2, last=True)
            move_hT(NB - 1)
            for p in range(2):
                move_h2(NB - 1, p, of=acc[:, 2:4, :] if p else turn)
                for h in range(HC):
                    gelu(NB - 1, p, h)

        @block.tensor
        def _(pe):
            pe.wait_ge(prep_step, 6)
            for c in range(KC):
                mm = pe.matmul(rowp[:, 0, 0:66], b1rep[:, c, :], wx[:, c, :], start=(c == 0), stop=(c == KC - 1))
            mm.then_inc(prep_sums, 1)
            pe.wait_ge(prep_step, 11)

            def project_x(b, u, k):
                pe.wait_ge(xT_ready, 4 * b + (k + 1))
                for c in range(KC):
                    mm = pe.matmul(rowp[:, u % 2, 66 * k:66 * k + 66], xT[:, k, P * c:P * c + P], wx[:, c, :],
                                   start=(k == 0 and c == 0), stop=(c == KC - 1), skip_group_check=True)
                if k == 3:
                    mm.then_inc(wh_done, 1)

            def piece(b, u, before):
                for k in range(4):
                    if k < 2:
                        pe.wait_ge(xhat_done, 2 * b + (k + 1))
                    else:
                        pe.wait_ge(xhat_act, 2 * b + (k - 1))
                    for c in range(KC):
                        at = 512 * k + P * c
                        mm = pe.transpose(turn[:, k % 2, P * c:P * c + P], xin[u][:, at:at + P], ident[:])
                    mm.then_inc(x_turned, 1)
                    if k:
                        project_x(b, u, k - 1)
                    elif before:
                        project_x(b - 1, u - 1, 3)
                if before:
                    pe.wait_ge(wh_ready, b)

            piece(0, 0, False)
            for u in range(1, 4):
                piece(u, u, True)
            with pe.Fori(1, 4) as i:
                for u in range(4):
                    piece(4 * i + u, u, True)
            project_x(NBL - 1, 3, 3)

            pe.wait_ge(wh_ready, NBL)
            for g in range(8):
                mm = pe.matmul(turn[:, 1, :], ones[:], whs[:, 8 * g:8 * g + 8, :].rearrange("p t f -> p (t f)"),
                               start=(g == 0), stop=(g == 7))
            mm.then_inc(wsum_done, 1)
            pe.wait_ge(s_landed, 16)
            pe.transpose(turn[:, 0, 0:NT], snat, ident[0:NT, 0:NT]).then_inc(s_turned, 1)

            def attend(n, b):
                if b == 0 and not (isinstance(n, int) and n == 0):
                    pe.wait_ge(evac_step, EV * n + (4 - EV))
                pe.wait_ge(mask_step, 48 * n + (3 * b + 3))
                pe.sem_inc(masks_taken, 1)
                if isinstance(n, int) and n == 0:
                    pe.wait_ge(uv_rest, 6 * (b // 4) + 6)
                for s in range(SUB):
                    for k in range(4):
                        c = 4 * b + k
                        pe.matmul(acc[:, s, 0:PART], eb[:, (b // 4) % 2, b % 4, P * s:P * s + P, k], uv[:, c, 0:PART],
                                  start=(c == 0), stop=(c == NT - 1), skip_group_check=True)
                        mm = pe.matmul(acc[:, s, PART:2 * PART], sbm[:, b % CR, P * s:P * s + P, k],
                                       uv[:, c, PART:2 * PART], start=False, stop=(c == NT - 1), skip_group_check=True)
                mm.then_inc(masks_used, 1)

            def turn_h(m):
                pe.wait_ge(evac_step, EV * m + EV)
                for s in range(SUB):
                    mm = pe.transpose(turn[:, 0, P * s:P * s + P], hcat[:, s, :].bitcast(F32), ident[:])
                mm.then_inc(h_turned, 1)

            def fc(m, p, to=rowp):
                pe.wait_ge(hT_ready, m + 1)
                if to is rowp and not (isinstance(m, int) and m == 0 and p == 0):
                    pe.wait_ge(out_added, 2 * m + p)
                for t in range(2):
                    rows = hT[:, P * (2 * p + t):P * (2 * p + t) + P]
                    pe.matmul(to[:, t, :], rows, fch[:], start=True, stop=False)
                    mm = pe.matmul(to[:, t, :], rows, fcl[:], start=False, stop=True)
                mm.then_inc(fc_done, 1)

            def turn_h2(m, p, to=turn):
                pe.wait_ge(ln_step, 2 * LN * m + (LN * p + LN))
                for c in range(KC):
                    for t in range(2):
                        at = 256 * (c % 2) + P * t
                        mm = pe.transpose(to[:, c // 2, at:at + P], xhat[:, t, P * c:P * c + P], ident[:])
                    if c % 2:
                        mm.then_inc(h2_turned, 1)

            def fc1(m, p, h):
                pe.wait_ge(h2l_ready, 4 * m + (2 * p + 2))
                for c in range(KC):
                    w, wl = w1h[:, c, P * h:P * h + P], w1l[:, c, P * h:P * h + P]
                    pe.matmul(turn[:, h % 2, 0:256], w, h2h[:, c, :], start=(c == 0), stop=False)
                    pe.matmul(turn[:, h % 2, 0:256], w, h2l[:, c, :], start=False, stop=False)
                    mm = pe.matmul(turn[:, h % 2, 0:256], wl, h2h[:, c, :], start=False, stop=(c == KC - 1))
                mm.then_inc(fc1_done, 1)

            def fc2(m, p, h):
                pe.wait_ge(m_ready, 16 * m + (8 * p + h + 1))
                for t in range(2):
                    hi, lo = m_h[:, h % 2, P * t:P * t + P], m_l[:, h % 2, P * t:P * t + P]
                    pe.matmul(rowp[:, t, :], hi, w2h[:, h, :], start=(h == 0), stop=False)
                    pe.matmul(rowp[:, t, :], hi, w2l[:, h, :], start=False, stop=False)
                    mm = pe.matmul(rowp[:, t, :], lo, w2h[:, h, :], start=False, stop=(h == HC - 1))
                if h == HC - 1:
                    mm.then_inc(fc2_done, 1)

            def rows(m, j, first=False):
                p, l = j // 8, j % 8
                if l == 0 and not (first and j == 0):
                    for h in (6, 7):
                        fc2(m if j else m - 1, 0 if j else 1, h)
                if j == 0:
                    turn_h(m)
                if l == 1:
                    fc(m, p)
                if l == 3:
                    turn_h2(m, p)
                if l == 4:
                    fc1(m, p, 0)
                    fc1(m, p, 1)
                if l >= 5:
                    for h in (2 * l - 10, 2 * l - 9):
                        fc2(m, p, h)
                        fc1(m, p, h + 2)

            def fc1_bias(j):
                pe.wait_ge(w_landed[j % 4], 16 * (j // 4 + 1))
                for i in range(4):
                    h = 4 * (j % 2) + i
                    mm = pe.matmul(rowp[:, 0, h:h + 1], xrows[:, j % 4, P * i:P * i + P], lnc[:, 3, j // 2:j // 2 + 1],
                                   start=(j == 0 and i == 0), stop=(j >= 6), skip_group_check=True)
                mm.then_inc(c1_done, 1)

            for b in range(16):
                if 1 <= b <= 8:
                    fc1_bias(b - 1)
                attend(0, b)
            pe.wait_ge(c1_ready, 1)
            for j in range(16):
                attend(1, j)
                if j == 4:
                    pe.wait_ge(w_low, 16)
                rows(0, j, first=True)
            with pe.Fori(2, NB) as n:
                for j in range(16):
                    attend(n, j)
                    rows(n - 1, j)
            m = NB - 1
            rows(m, 0)
            fc(m, 0)
            fc(m, 1, to=acc[:, 0:2, :])
            turn_h2(m, 0)
            for j in range(4, 8):
                rows(m, j)
                if j == 6:
                    turn_h2(m, 1, to=acc[:, 2:4, :])
            fc2(m, 0, 6)
            fc2(m, 0, 7)
            rows(m, 12)
            pe.wait_ge(out_added, 2 * m + 1)
            for j in range(13, 16):
                rows(m, j)
            fc2(m, 1, 6)
            fc2(m, 1, 7)

        @block.vector
        def _(dve):

            def stats(b, i, u):
                dve.wait_ge(xin_landed[u], 64 * i + 64)
                for k in range(4):
                    last = dve.bn_stats(stat[:, k, :], xin[u][:, D * k:D * k + D])
                last.then_inc(stats_step, 1)
                dve.wait_ge(stats_step, b + 1)
                dve.sem_inc(aggr_begun, 1)
                for k in range(4):
                    last = dve.bn_aggr(mv[:, u % 2, k, :], stat[:, k, :])
                last.then_inc(stats_done, 1)
                dve.wait_ge(stats_done, b + 1)

            stats(0, 0, 0)
            dve.wait_ge(const_made, 2)
            dve.wait_ge(const_landed, CONSTS)
            prep = Steps(dve, prep_step, 0)
            prep.did(dve.tensor_copy(wx[:, :, 0:F], wraw))
            for i in range(2):
                prep.did(dve.tensor_tensor(wprod, wraw, a_bc[:, F * i:F * i + F].unsqueeze(1).to_broadcast([P, KC, F]),
                                           ALU.mult))
                prep.wait()
                prep.did(dve.tensor_reduce(wx[:, :, F + i:F + i + 1], wprod, AX_X, ALU.add))
                prep.wait()
            for c in range(KC):
                last = dve.tensor_scalar(b1rep[:, c, :], ones[:], lnc[:, 1, c:c + 1], None, ALU.mult)
            prep.did(last)
            dve.wait_ge(prep_sums, 1)
            prep.did(dve.tensor_copy(crow, rowp[:, 0, 0:66]))
            for c in range(KC):
                prep.did(dve.tensor_scalar(wx[:, c, :], wx[:, c, :], lnc[:, 0, c:c + 1], None, ALU.mult))
            def normalise(b, u):
                dve.wait_ge(rstd_ready, b + 1)
                for k in range(2):
                    xt = xin[u][:, D * k:D * k + D]
                    dve.tensor_scalar(xt, xt, mv[:, u % 2, k, 0:1], rstd[:, u % 2, k:k + 1], ALU.subtract, ALU.mult)\
                       .then_inc(xhat_done, 1)

            def keep_wh(b, u):
                dve.wait_ge(wh_done, b + 1)
                got = rowp[:, u % 2, 0:264].rearrange("p (k f) -> p k f", k=4)
                dve.tensor_tensor(whs[:, bass.ds(4 * b, 4), :], got[:, :, 0:F],
                                  crow[:, 0:F].unsqueeze(1).to_broadcast([P, 4, F]), ALU.add)
                dve.tensor_scalar(s_tab[:, bass.ds(4 * b, 4)], got[:, :, F], crow[:, F:F + 1], None, ALU.add)
                dve.tensor_scalar(d_tab[:, bass.ds(4 * b, 4)], got[:, :, F + 1], crow[:, F + 1:F + 2], None,
                                  ALU.add).then_inc(wh_ready, 1)

            def split_fc():
                dve.wait_ge(late_landed, 16 * 5)
                dve.tensor_copy(fch[:], fcs).then_inc(fc_high, 1)
                dve.wait_ge(fc_high, 1)
                dve.tensor_tensor(fcl[:], fcs, fch[:].bitcast(F32), ALU.subtract)

            for u in range(4):
                normalise(u, u)
                if u == 0:
                    stats(1, 0, 1)
                    split_fc()
                stats(u + 2, (u + 2) // 4, (u + 2) % 4)
                if u:
                    keep_wh(u - 1, u - 1)
            with dve.Fori(1, 3) as i:
                for u in range(4):
                    b = 4 * i + u
                    normalise(b, u)
                    stats(b + 2, i + (u + 2) // 4, (u + 2) % 4)
                    keep_wh(b - 1, (u - 1) % 4)
            for u in range(4):
                b = 12 + u
                normalise(b, u)
                if u < 2:
                    stats(b + 2, 3, u + 2)
                keep_wh(b - 1, (u - 1) % 4)
            keep_wh(15, 3)
            dve.wait_ge(wh_ready, NBL)

            tab = Steps(dve, table_step, 0)
            tab.did(dve.tensor_reduce(dmax[:, 0:1], d_tab[:], AX_X, ALU.max))
            tab.did(dve.tensor_scalar(nd_tab[:], d_tab[:], -1.0, None, ALU.mult))
            dve.wait_ge(dmax_ready, 1)
            tab.did(dve.tensor_scalar(dmax[:, 2:3], dmax[:, 1:2], -1.0, HEADROOM, ALU.mult, ALU.add))
            tab.did(dve.tensor_scalar(dmax[:, 3:4], dmax[:, 1:2], -SLOPE, HEADROOM, ALU.mult, ALU.add))

            def uv_rows(st):
                for t in range(3):
                    for v in range(2):
                        us = u_tab[:, 16 * st:16 * st + 16, v:v + 1]
                        if t == 0:
                            dve.tensor_copy(uf[v][:, :, F:C1], us)
                            dve.tensor_tensor(uf[v][:, :, 0:F], whs[:, 16 * st:16 * st + 16, :],
                                              us.to_broadcast([P, 16, F]), ALU.mult).then_inc(uv_rest, 1)
                        else:
                            c = PART * v + C1 * (t - 1)
                            dve.wait_ge(uv_part, 4 * st + 2 * t + v - 1)
                            rest = uf[v] if t == 1 else uv[:, 16 * st:16 * st + 16, c + C1:c + 2 * C1]
                            dve.tensor_tensor(rest, uf[v], uv[:, 16 * st:16 * st + 16, c:c + C1], ALU.subtract)\
                               .then_inc(uv_rest, 1)
                dve.wait_ge(uv_rest, 6 * st + 6)

            def row_tables():
                dve.wait_ge(s_turned, 1)
                tab.did(dve.tensor_scalar(t_tab, turn[:, 0, 0:NT], dmax[:, 1:2], None, ALU.add))
                tab.wait()
                tab.did(dve.scalar_tensor_tensor(lt_tab, t_tab, SLOPE, t_tab, ALU.mult, ALU.max))
                tab.wait()
                tab.did(dve.tensor_tensor(ab_tab[:, :, 0], t_tab, lt_tab, ALU.subtract))
                tab.did(dve.scalar_tensor_tensor(ab_tab[:, :, 1], t_tab, SLOPE, lt_tab, ALU.mult, ALU.subtract))
                tab.did(dve.tensor_reduce(wsum[:], turn[:, 1, :].rearrange("p (t f) -> p f t", f=F), AX_X, ALU.add))

            def turn_piece(n, i):
                st = i // SUB
                dve.wait_ge(bytes_ready, 16 * n + (i + 1))
                if i % SUB == 0 and not (isinstance(n, int) and 16 * n + 4 * st < 8):
                    dve.wait_ge(masks_used, 16 * n + (4 * st - 4))
                g = 4 * (i % SUB)
                dst = edges[:, st % 2, :].rearrange("p (b g r) -> p g b r", b=4, r=Q)[:, g:g + 4, :, :]
                dve.transpose(dst, byte_ring[:, i % BYTES, :].bitcast(U32).rearrange("p (g b w) -> p g b w", g=4, b=4))\
                   .then_inc(turned, 1)

            def own_signs(n, b):
                if not (isinstance(n, int) and 16 * n + b < CR):
                    dve.wait_ge(masks_used, 16 * n + (b + 1 - CR))
                if b == 0:
                    dve.wait_ge(srow_landed, 16 * n + 16)
                for k in range(act_chunks(n, b).start):
                    last = dve.tensor_scalar(sbu[:, b % CR, :, k], srows[:, n % 2, :], nd_tab[:, 4 * b + k:4 * b + k + 1],
                                             float(EDGE_BYTE), ALU.is_lt, ALU.mult)
                last.then_inc(mask_step, 1)

            def masks(n, b, signs_made=False):
                if not signs_made:
                    own_signs(n, b)
                at = 48 * n + 3 * b
                st = b // 4
                e = edges[:, st % 2, 512 * (b % 4):512 * (b % 4) + 512]
                sg = signs[:, b % CR, :]
                if b % 4 == 0:
                    dve.wait_ge(turned, 16 * n + (4 * st + 4))
                dve.wait_ge(act_signs, 16 * n + (b + 1))
                dve.wait_ge(mask_step, at + 1)
                dve.scalar_tensor_tensor(sg, e, EDGE_WORD, sg, ALU.bitwise_and, ALU.bitwise_and).then_inc(mask_step, 1)
                dve.wait_ge(mask_step, at + 2)
                dve.scalar_tensor_tensor(e, e, EDGE_WORD, sg, ALU.bitwise_and, ALU.bitwise_xor).then_inc(mask_step, 1)

            def sum_parts(m):
                ev = Steps(dve, evac_step, EV * m)
                dve.wait_ge(masks_used, 16 * m + 16)
                for s in range(SUB):
                    ev.did(dve.tensor_reduce(red[:, s, :, :], accp[:, s, :, :, :], AX_X, ALU.add))

            def attention_rows(m):
                ev = Steps(dve, evac_step, EV * m + SUB)
                ev.wait()
                ab = ab_tab[:, bass.ds(4 * m, 4), :].unsqueeze(3).to_broadcast([P, SUB, 2, C1])
                ev.did(dve.tensor_tensor(red, red, ab, ALU.mult))
                ev.wait()
                ev.did(dve.tensor_tensor(num, red[:, :, 0, :], red[:, :, 1, :], ALU.add))
                ev.wait()
                none, total, inverse = den[:, 0, :], den[:, 1, :], den[:, 2, :]
                ev.did(dve.tensor_scalar(none, num[:, :, F], 0.0, None, ALU.is_equal))
                ev.wait()
                ev.did(dve.scalar_tensor_tensor(total, none, float(N), num[:, :, F], ALU.mult, ALU.add))
                ev.wait()
                ev.did(dve.reciprocal(inverse, total))
                ev.did(dve.tensor_tensor(hp, none.unsqueeze(2).to_broadcast([P, SUB, F]),
                                         wsum[:].unsqueeze(1).to_broadcast([P, SUB, F]), ALU.mult))
                ev.wait()
                ev.did(dve.tensor_tensor(num[:, :, 0:F], num[:, :, 0:F], hp, ALU.add))
                ev.wait()
                ev.did(dve.tensor_tensor(hp, num[:, :, 0:F], inverse.unsqueeze(2).to_broadcast([P, SUB, F]), ALU.mult))
                ev.wait()
                ev.did(dve.tensor_copy(hcat[:, :, 0:F], hp))
                ev.wait()
                ev.did(dve.tensor_tensor(hcat[:, :, F:2 * F], hp, hcat[:, :, 0:F].bitcast(F32), ALU.subtract))

            def add_out(m, p):
                dve.wait_ge(out_biased, 2 * m + (p + 1))
                dve.wait_ge(fc2_done, 2 * m + (p + 1))
                xr = xrows[:, 2 * p:2 * p + 2, :]
                dve.tensor_tensor(xr, rowp[:, :, :], xr, ALU.add).then_inc(out_added, 1)

            def add_attention(m, p, of=rowp):
                ln = Steps(dve, ln_step, 2 * LN * m + LN * p)
                dve.wait_ge(fc_done, 2 * m + (p + 1))
                dve.wait_ge(x_biased, 2 * m + (p + 1))
                xr = xrows[:, 2 * p:2 * p + 2, :]
                ln.did(dve.tensor_tensor(xr, of[:, 0:2, :], xr, ALU.add))
                ln.wait()
                for t in range(2):
                    ln.did(dve.bn_stats(stat[:, t, :], xrows[:, 2 * p + t, :]))
                ln.wait()
                dve.sem_inc(aggr_begun, 1)
                for t in range(2):
                    ln.did(dve.bn_aggr(mv2[:, t, :], stat[:, t, :]))

            def normalise2(m, p):
                ln = Steps(dve, ln_step, 2 * LN * m + (LN * p + 5))
                dve.wait_ge(rstd2_ready, 2 * m + (p + 1))
                for t in range(2):
                    ln.did(dve.tensor_scalar(xhat[:, t, :], xrows[:, 2 * p + t, :], mv2[:, t, 0:1], rstd2[:, t:t + 1],
                                             ALU.subtract, ALU.mult))

            def low_h2(m, p, of=turn):
                for c in range(2):
                    dve.wait_ge(h2h_ready, 4 * m + (2 * p + c + 1))
                    dve.tensor_tensor(h2l[:, 2 * c:2 * c + 2, :].rearrange("p c i -> p (c i)"), of[:, c, :],
                                      h2h[:, 2 * c:2 * c + 2, :].rearrange("p c i -> p (c i)").bitcast(F32),
                                      ALU.subtract).then_inc(h2l_ready, 1)

            def low_m(m, p, h):
                dve.wait_ge(gelu_done, 16 * m + (8 * p + h + 1))
                dve.tensor_tensor(m_l[:, h % 2, :], m_f[:, h % 2, :], m_h[:, h % 2, :].bitcast(F32), ALU.subtract)\
                   .then_inc(m_ready, 1)

            def slot(n, j, m=None, first=False, last=False):
                p, l = j // 8, j % 8

                def turn(*ahead):
                    for i in ahead:
                        if n is not None and not (last and j + i >= 16):
                            turn_piece(n + (j + i) // 16, (j + i) % 16)

                def mask(*ahead):
                    for i in ahead:
                        if n is not None and not (last and j + i >= 16):
                            masks(n + (j + i) // 16, (j + i) % 16)

                if l == 0:
                    if j and m is not None:
                        mask(3)
                        turn(4)
                        add_out(m, 0)
                        turn(5)
                    else:
                        if m is not None and not first:
                            add_out(m - 1, 1)
                        turn(4, 5)
                        mask(3)
                if l == 1:
                    if j == 9:
                        if n is not None:
                            own_signs(n, j + 3)
                        turn(5)
                    if m is not None:
                        add_attention(m, p)
                    if j == 1:
                        if n is not None:
                            own_signs(n, j + 3)
                        turn(5)
                if l == 2:
                    if j == 10:
                        turn(5)
                    if m is not None:
                        normalise2(m, p)
                    if j == 2:
                        turn(5)
                    if n is not None:
                        masks(n, j + 2, signs_made=True)
                if l == 3:
                    if m is not None:
                        low_h2(m, p)
                    mask(2)
                if l == 4:
                    turn(4, 5)
                    mask(2)
                    if m is not None:
                        low_m(m, p, 0)
                    mask(3)
                    if m is not None:
                        low_m(m, p, 1)
                if l == 5:
                    turn(5, 6)
                if j == 15 and n is not None and m is None:
                    sum_parts(n)
                if l >= 5:
                    mask(3)
                if j == 15 and n is not None and m is not None:
                    sum_parts(n)
                if l >= 5 and m is not None:
                    low_m(m, p, 2 * l - 8)
                    low_m(m, p, 2 * l - 7)

            dve.wait_ge(exps_done, 1)
            uv_rows(0)
            uv_rows(1)
            dve.wait_ge(wsum_done, 1)
            turn_piece(0, 0)
            turn_piece(0, 1)
            uv_rows(2)
            turn_piece(0, 2)
            turn_piece(0, 3)
            masks(0, 0)
            row_tables()
            masks(0, 1)
            masks(0, 2)
            uv_rows(3)
            for j in range(16):
                slot(0, j)
                if j == 9:
                    dve.wait_ge(c1_done, 8)
                    dve.tensor_tensor(c1[:], rowp[:, 0, 0:HC], b1c[:], ALU.add).then_inc(c1_ready, 1)
            dve.wait_ge(exps_done, 2)
            attention_rows(0)
            for j in range(16):
                slot(1, j, m=0, first=True)
            attention_rows(1)
            with dve.Fori(2, NB - 1) as n:
                for j in range(16):
                    slot(n, j, m=n - 1)
                attention_rows(n)
            for j in range(16):
                slot(NB - 1, j, m=NB - 2, last=True)
            attention_rows(NB - 1)
            m = NB - 1
            add_out(m - 1, 1)
            add_attention(m, 0)
            normalise2(m, 0)
            low_h2(m, 0)
            for h in range(HC):
                low_m(m, 0, h)
                if h == 1:
                    add_attention(m, 1, of=acc)
                if h == 3:
                    normalise2(m, 1)
            low_h2(m, 1, of=acc[:, 2:4, :])
            add_out(m, 0)
            for h in range(HC):
                low_m(m, 1, h)
            add_out(m, 1)


_INS = ["x", "adj", "W", "a", "fc_wT", "fc_b", "ln1_g", "ln1_b", "ln2_g", "ln2_b", "fc1_wT", "fc1_b", "fc2_wT", "fc2_b"]


def kernel(x, adj, L0_gnn_W, L0_gnn_a, L0_gnn_fc_w, L0_gnn_fc_b, L0_gnn_ln1_g, L0_gnn_ln1_b, L0_gnn_ln2_g,
           L0_gnn_ln2_b, L0_gnn_fc1_w, L0_gnn_fc1_b, L0_gnn_fc2_w, L0_gnn_fc2_b):
    import numpy as np
    import concourse.bacc as bacc
    from concourse import mybir
    from concourse.bass_utils import run_bass_kernel_spmd

    def columns(v):
        return np.asarray(v).reshape(-1, 128).T

    given = dict(
        x=x, adj=adj, W=L0_gnn_W, a=np.asarray(L0_gnn_a).reshape(1, -1),
        fc_wT=np.asarray(L0_gnn_fc_w).T, fc_b=np.asarray(L0_gnn_fc_b).reshape(1, -1),
        ln1_g=columns(L0_gnn_ln1_g), ln1_b=columns(L0_gnn_ln1_b),
        ln2_g=columns(L0_gnn_ln2_g), ln2_b=columns(L0_gnn_ln2_b),
        fc1_wT=np.asarray(L0_gnn_fc1_w).T, fc1_b=columns(L0_gnn_fc1_b),
        fc2_wT=np.asarray(L0_gnn_fc2_w).T, fc2_b=np.asarray(L0_gnn_fc2_b).reshape(1, -1),
    )
    nc = bacc.Bacc("TRN2", target_bir_lowering=False, num_devices=1)
    arrays, args = {}, []
    for name in _INS:
        v = np.ascontiguousarray(given[name])
        arrays[f"in_{name}"] = v
        args.append(nc.dram_tensor(f"in_{name}", v.shape, mybir.dt.from_np(v.dtype), kind="ExternalInput").ap())
    args.append(nc.dram_tensor("out_rows", arrays["in_x"].shape, mybir.dt.float32, kind="ExternalOutput").ap())
    gat_layer(nc, *args)
    got = run_bass_kernel_spmd(nc, [arrays], core_ids=[0])
    return got.results[0]["out_rows"]
```
